# Optimizing a Trainium2 kernel written in Bass

```python
import numpy as np
import jax
import jax.numpy as jnp

def _softmax(x, axis=-1):
    return jax.nn.softmax(x, axis=axis)

def _gelu(x):
    return jax.nn.gelu(x, approximate=True)

def _silu(x):
    return jax.nn.silu(x)

def _sigmoid(x):
    return jax.nn.sigmoid(x)

def _layernorm(x, axis=-1, eps=1e-05):
    m = jnp.mean(x, axis=axis, keepdims=True)
    v = jnp.var(x, axis=axis, keepdims=True)
    return (x - m) / jnp.sqrt(v + eps)

def _scatter_add(tgt, idx, src, axis=0):
    return tgt.at[idx].add(src)

def _segment_sum(src, seg, n):
    return jax.ops.segment_sum(src, seg, n)
kernel_name = 'mk_prb_d1_jaxref_r8_717325'

def setup_inputs(seed: int=0):
    np.random.seed(seed)
    _w = jnp.asarray

    def _L0_attn_setup():
        import jax, jax.numpy as jnp
        import numpy as np
        B, S, D, H = (2, 256, 128, 16)
        HD = D // H
        EPS = 1e-05
        THETA = 10000.0

        def _rope_freqs(seq_len, dim, dtype=jnp.float32):
            inv_freq = 1.0 / THETA ** (np.arange(0, dim, 2)[:dim // 2] / dim)
            t = np.arange(seq_len)
            freqs = np.outer(t, inv_freq)
            return (jnp.asarray(np.cos(freqs), dtype), jnp.asarray(np.sin(freqs), dtype))

        def _apply_rope(x, cos, sin):
            x_even = x[..., 0::2]
            x_odd = x[..., 1::2]
            cos = cos.reshape(1, x.shape[1], 1, -1)
            sin = sin.reshape(1, x.shape[1], 1, -1)
            out_even = x_even * cos - x_odd * sin
            out_odd = x_even * sin + x_odd * cos
            return jnp.stack([out_even, out_odd], axis=-1).reshape(x.shape)
        key = jax.random.key(seed)
        ks = jax.random.split(key, 6)
        s = 1.0 / np.sqrt(D)
        return {'x': jax.random.normal(ks[0], (B, S, D), jnp.float32), 'Wq': jax.random.normal(ks[1], (D, D), jnp.float32) * s, 'Wk': jax.random.normal(ks[2], (D, D), jnp.float32) * s, 'Wv': jax.random.normal(ks[3], (D, D), jnp.float32) * s, 'Wo': jax.random.normal(ks[4], (D, D), jnp.float32) * s, 'alpha': jnp.ones((1,), jnp.float32)}
    _L0_attn_in = _L0_attn_setup()

    def _L0_ffn_setup():
        import jax, jax.numpy as jnp
        import numpy as np
        B, S, D = (1, 256, 128)
        E, K, F = (64, 8, 96)
        SF = 96
        C = 64
        ROUTED_SCALE = 1.0

        def _moe_forward(x, router_w, w_gate, w_up, w_down, ws_gate_up, ws_down):
            T = x.shape[0]
            logits = x.astype(jnp.float32) @ router_w.T
            probs = jax.nn.softmax(logits, axis=-1)
            topk_w, topk_ids = jax.lax.top_k(probs, K)
            topk_w = topk_w / jnp.sum(topk_w, axis=-1, keepdims=True)
            topk_w = topk_w.astype(x.dtype)
            N = T * K
            flat_e = topk_ids.reshape(-1)
            flat_w = topk_w.reshape(-1)
            tok = jnp.arange(N) // K
            onehot = flat_e[:, None] == jnp.arange(E)[None, :]
            pos = jnp.cumsum(onehot, axis=0)[jnp.arange(N), flat_e] - 1
            valid = pos < C
            idx = jnp.where(valid, flat_e * C + pos, E * C)
            x_buf = jnp.zeros((E * C + 1, x.shape[1]), x.dtype).at[idx].set(x[tok])
            xb = x_buf[:E * C].reshape(E, C, -1)
            g = jnp.einsum('ecd,edf->ecf', xb, w_gate)
            u = jnp.einsum('ecd,edf->ecf', xb, w_up)
            h = jax.nn.silu(g) * u
            y = jnp.einsum('ecf,efd->ecd', h, w_down).reshape(E * C, -1)
            safe = jnp.where(valid, idx, 0)
            contrib = y[safe] * (flat_w * valid.astype(flat_w.dtype))[:, None]
            routed = jax.ops.segment_sum(contrib, tok, num_segments=T)
            routed = routed * ROUTED_SCALE
            gu = x @ ws_gate_up
            sg, su = (gu[:, :SF], gu[:, SF:])
            shared = jax.nn.silu(sg) * su @ ws_down
            return routed + shared
        key = jax.random.key(seed)
        ks = jax.random.split(key, 7)
        w = 0.02
        return {'hidden_states': jax.random.normal(ks[0], (B, S, D), jnp.float32), 'router_w': jax.random.normal(ks[1], (E, D), jnp.float32) * w, 'w_gate': jax.random.normal(ks[2], (E, D, F), jnp.float32) * w, 'w_up': jax.random.normal(ks[3], (E, D, F), jnp.float32) * w, 'w_down': jax.random.normal(ks[4], (E, F, D), jnp.float32) * w, 'ws_gate_up': jax.random.normal(ks[5], (D, 2 * SF), jnp.float32) * w, 'ws_down': jax.random.normal(ks[6], (SF, D), jnp.float32) * w}
    _L0_ffn_in = _L0_ffn_setup()
    _d = {'L0_attn_x': _L0_attn_in['x'], 'L0_attn_Wq': _L0_attn_in['Wq'], 'L0_attn_Wk': _L0_attn_in['Wk'], 'L0_attn_Wv': _L0_attn_in['Wv'], 'L0_attn_Wo': _L0_attn_in['Wo'], 'L0_attn_alpha': _L0_attn_in['alpha'], 'L0_ffn_router_w': _L0_ffn_in['router_w'], 'L0_ffn_w_gate': _L0_ffn_in['w_gate'], 'L0_ffn_w_up': _L0_ffn_in['w_up'], 'L0_ffn_w_down': _L0_ffn_in['w_down'], 'L0_ffn_ws_gate_up': _L0_ffn_in['ws_gate_up'], 'L0_ffn_ws_down': _L0_ffn_in['ws_down']}
    _x0 = _d['L0_attn_x']
    _d['L0_attn_x'] = jax.random.normal(jax.random.fold_in(jax.random.key(seed), 1), (4, 1024, 128), dtype=_x0.dtype)
    del _x0
    return _d

def reference(L0_attn_x, L0_attn_Wq, L0_attn_Wk, L0_attn_Wv, L0_attn_Wo, L0_attn_alpha, L0_ffn_router_w, L0_ffn_w_gate, L0_ffn_w_up, L0_ffn_w_down, L0_ffn_ws_gate_up, L0_ffn_ws_down):

    def _L0_attn_ref(x, Wq, Wk, Wv, Wo, alpha):
        import jax, jax.numpy as jnp
        import numpy as np
        B, S, D, H = (2, 256, 128, 16)
        HD = D // H
        EPS = 1e-05
        THETA = 10000.0

        def _rope_freqs(seq_len, dim, dtype=jnp.float32):
            inv_freq = 1.0 / THETA ** (np.arange(0, dim, 2)[:dim // 2] / dim)
            t = np.arange(seq_len)
            freqs = np.outer(t, inv_freq)
            return (jnp.asarray(np.cos(freqs), dtype), jnp.asarray(np.sin(freqs), dtype))

        def _apply_rope(x, cos, sin):
            x_even = x[..., 0::2]
            x_odd = x[..., 1::2]
            cos = cos.reshape(1, x.shape[1], 1, -1)
            sin = sin.reshape(1, x.shape[1], 1, -1)
            out_even = x_even * cos - x_odd * sin
            out_odd = x_even * sin + x_odd * cos
            return jnp.stack([out_even, out_odd], axis=-1).reshape(x.shape)
        b, s, d = x.shape
        q = (x @ Wq).reshape(b, s, H, HD)
        k = (x @ Wk).reshape(b, s, H, HD)
        v = (x @ Wv).reshape(b, s, H, HD)
        cos, sin = _rope_freqs(s, HD, x.dtype)
        q = _apply_rope(q, cos, sin)
        k = _apply_rope(k, cos, sin)
        qk = jnp.einsum('bqhd,bkhd->bhqk', q, k)
        qn = jnp.sum(q * q, axis=-1)
        kn = jnp.sum(k * k, axis=-1)
        dist2 = qn.transpose(0, 2, 1)[:, :, :, None] + kn.transpose(0, 2, 1)[:, :, None, :] - 2.0 * qk
        scores = qk * qk / (dist2 + EPS)
        scale = (jnp.sqrt(jnp.float32(HD)) / jnp.log(jnp.float32(1 + HD))) ** alpha[0]
        scores = scores * scale
        causal = jnp.tril(jnp.ones((s, s), bool))
        big_neg = jnp.finfo(scores.dtype).min
        scores = jnp.where(causal[None, None, :, :], scores, big_neg)
        attn = jax.nn.softmax(scores, axis=-1)
        out = jnp.einsum('bhqk,bkhd->bqhd', attn, v).reshape(b, s, d)
        return out @ Wo

    def _L0_ffn_ref(hidden_states, router_w, w_gate, w_up, w_down, ws_gate_up, ws_down):
        import jax, jax.numpy as jnp
        import numpy as np
        B, S, D = (1, 256, 128)
        E, K, F = (64, 8, 96)
        SF = 96
        C = 64
        ROUTED_SCALE = 1.0

        def _moe_forward(x, router_w, w_gate, w_up, w_down, ws_gate_up, ws_down):
            T = x.shape[0]
            logits = x.astype(jnp.float32) @ router_w.T
            probs = jax.nn.softmax(logits, axis=-1)
            topk_w, topk_ids = jax.lax.top_k(probs, K)
            topk_w = topk_w / jnp.sum(topk_w, axis=-1, keepdims=True)
            topk_w = topk_w.astype(x.dtype)
            N = T * K
            flat_e = topk_ids.reshape(-1)
            flat_w = topk_w.reshape(-1)
            tok = jnp.arange(N) // K
            onehot = flat_e[:, None] == jnp.arange(E)[None, :]
            pos = jnp.cumsum(onehot, axis=0)[jnp.arange(N), flat_e] - 1
            valid = pos < C
            idx = jnp.where(valid, flat_e * C + pos, E * C)
            x_buf = jnp.zeros((E * C + 1, x.shape[1]), x.dtype).at[idx].set(x[tok])
            xb = x_buf[:E * C].reshape(E, C, -1)
            g = jnp.einsum('ecd,edf->ecf', xb, w_gate)
            u = jnp.einsum('ecd,edf->ecf', xb, w_up)
            h = jax.nn.silu(g) * u
            y = jnp.einsum('ecf,efd->ecd', h, w_down).reshape(E * C, -1)
            safe = jnp.where(valid, idx, 0)
            contrib = y[safe] * (flat_w * valid.astype(flat_w.dtype))[:, None]
            routed = jax.ops.segment_sum(contrib, tok, num_segments=T)
            routed = routed * ROUTED_SCALE
            gu = x @ ws_gate_up
            sg, su = (gu[:, :SF], gu[:, SF:])
            shared = jax.nn.silu(sg) * su @ ws_down
            return routed + shared
        b, s, d = hidden_states.shape
        x = hidden_states.reshape(-1, d)
        out = _moe_forward(x, router_w, w_gate, w_up, w_down, ws_gate_up, ws_down)
        return out.reshape(b, s, d)
    x = L0_attn_x
    xn = _layernorm(x, axis=-1)
    x = x + _L0_attn_ref(xn, L0_attn_Wq, L0_attn_Wk, L0_attn_Wv, L0_attn_Wo, L0_attn_alpha) + _L0_ffn_ref(xn, L0_ffn_router_w, L0_ffn_w_gate, L0_ffn_w_up, L0_ffn_w_down, L0_ffn_ws_gate_up, L0_ffn_ws_down)
    return x

_drawn_inputs = setup_inputs


def setup_inputs(seed=0):
    import zlib

    import numpy as np

    out = dict(_drawn_inputs(seed))
    spreads = {}
    factors = {'L0_ffn_router_w': 8.0,
     'L0_ffn_w_gate': 8.0,
     'L0_ffn_w_up': 8.0,
     'L0_ffn_w_down': 8.0,
     'L0_ffn_ws_gate_up': 8.0,
     'L0_ffn_ws_down': 8.0}
    for name, (base, spread) in spreads.items():
        noise = np.random.default_rng([zlib.crc32(name.encode()), seed]).standard_normal(out[name].shape)
        drawn = base * np.exp(spread * noise) if base else spread * noise
        out[name] = jnp.asarray(drawn.astype(out[name].dtype))
    for name, factor in factors.items():
        out[name] = (out[name] * factor).astype(out[name].dtype)
    return out
```

```python
from contextlib import ExitStack

import numpy as np
import concourse.bass as bass
from concourse import mybir

F32 = mybir.dt.float32
BF16 = mybir.dt.bfloat16
I32 = mybir.dt.int32
ALU = mybir.AluOpType
ACT = mybir.ActivationFunctionType
AXX = mybir.AxisListType.X

P = 128
B, S, D = 4, 1024, 128
T = B * S
H, HD = 16, 8
E, TOPK, F = 64, 8, 96
SLOTS = 64
ATT_EPS = 1e-5
LN_EPS = 1e-5
TILES = T // P
CH = 512
NCH = T // CH
NPART = 3
GH = 4
QT = S // P
TRIPS = B * H // (2 * GH)
PROD = NPART * NPART * HD
NORM_K = PROD
NORM_Q = 96
DUMMY = SLOTS
ROW = D + E
MASK_D = -1e18
MASK_T = -1e30
ACT_SET = "natural_log_exp_and_others"


def ge(eng, sem, value):
    if isinstance(value, int) and value <= 0:
        return
    eng.wait_ge(sem, value)


def wait_apart(eng, sem, value, passed):
    ge(eng, sem, value)
    eng.sem_inc(passed, 1)


def step_list():
    out = []
    for i in reversed(range(QT)):
        w = P * (i + 1)
        n = 1 if w > 512 else 2 if w > 256 else 4
        pitch = w if n != 2 else 512
        out += [(i, list(range(c, c + n)), pitch) for c in range(0, GH, n)]
    return out


STEPS = step_list()
NS = len(STEPS)
NT = 2 * NS
ROUTE = 19
LEAD = 3


def value_work():
    work = [[] for _ in range(NS)]
    for i in range(QT):
        at = [n for n in range(NS) if STEPS[n][0] == (i - 1 if i else 0)]
        for a, n in enumerate(at):
            work[n].append((i, (i + 1) * a // len(at), (i + 1) * (a + 1) // len(at)))
    return [sorted(w, reverse=True) for w in work]


VALUES = value_work()
HALF_END = [max(n for n in range(NS) if any(w[0] == i for w in VALUES[n])) for i in (QT // 2, 0)]


def program(nc, x, wq, wqs, wk, wks, wv, wo, alpha, rwt, wgu, wdn, wsgu, wsdn, consts, rope, out):
    with ExitStack() as ctx:
        def sb(name, shape, dt=F32, c=ctx):
            return c.enter_context(nc.sbuf_tensor(name, shape, dt))

        def ps(name, shape, c):
            return c.enter_context(nc.psum_tensor(name, shape, F32))

        def sem(name, c=ctx):
            return c.enter_context(nc.semaphore(name))

        qk_parts = nc.dram_tensor("qk_parts", [TRIPS, 2, 8, NPART * HD, S], BF16, kind="Internal").ap()
        nrm_parts = nc.dram_tensor("nrm_parts", [TRIPS, 2, 8, NPART, S], BF16, kind="Internal").ap()
        rows = nc.dram_tensor("rows", [T + DUMMY, ROW], F32, kind="Internal").ap()
        routed = nc.dram_tensor("routed", [T + DUMMY, D], F32, kind="Internal").ap()
        xT_d = nc.dram_tensor("xT_d", [P, T], F32, kind="Internal").ap()
        att_d = nc.dram_tensor("att_d", [TRIPS, 2, GH * HD, S], F32, kind="Internal").ap()

        ident = sb("ident", [P, P])
        identb = sb("identb", [P, P], BF16)
        mask_d = sb("mask_d", [P, P], BF16)
        mask_t = sb("mask_t", [P, P], BF16)
        cst = sb("cst", [P, consts.shape[1]])
        scale = sb("scale", [P, 1])
        v_all = sb("v_all", [P, TRIPS, QT, 64])
        idx64 = sb("idx64", [SLOTS, E], I32)
        idxp = sb("idxp", [P, E // 2], I32)
        q_d = sb("q_d", [P, 2, GH, S], BF16)
        q_s = sb("q_s", [P, 2, GH, S], BF16)
        k_t = sb("k_t", [P, 2, GH, S], BF16)
        C_MD, C_MT, C_NB, C_TV, C_SI = 128, 256, 384, 416, 448

        with ExitStack() as pc:
            x_all = sb("x_all", [P, TILES, D], F32, pc)
            w_q = sb("w_q", [P, D], F32, pc)
            w_qs = sb("w_qs", [P, D], F32, pc)
            w_k = sb("w_k", [P, D], F32, pc)
            w_ks = sb("w_ks", [P, D], F32, pc)
            w_v = sb("w_v", [P, D], F32, pc)
            w_r = sb("w_r", [P, E], F32, pc)
            tabs = sb("tabs", [P, 2, S], F32, pc)
            zero = sb("zero", [P, 13 * D], F32, pc)
            st6 = sb("st6", [P, TILES, 6], F32, pc)
            mv = sb("mv", [P, TILES, 2], F32, pc)
            rstd = sb("rstd", [P, TILES], F32, pc)
            al = sb("al", [P, 1], F32, pc)
            xn = sb("xn", [P, 2, 4, D], F32, pc)
            xT = sb("xT", [P, 2, CH], F32, pc)
            ra = sb("ra", [P, 2, CH], F32, pc)
            rb = sb("rb", [P, 2, CH], F32, pc)
            qf = sb("qf", [P, 2, CH], F32, pc)
            res = sb("res", [P, 2, CH], F32, pc)
            sq = sb("sq", [P, 2, CH], F32, pc)
            parts = sb("parts", [P, 2, 2, NPART, CH], BF16, pc)
            nf = sb("nf", [64, CH], F32, pc)
            nres = sb("nres", [64, CH], F32, pc)
            nparts = sb("nparts", [64, 2, NPART, CH], BF16, pc)
            nmax = sb("nmax", [P, 4], F32, pc)
            pe_ = sb("pexp", [P, 4, E], F32, pc)
            top8 = sb("top8", [P, 4, 8], F32, pc)
            mr = sb("mr", [P, 4, E], F32, pc)
            sel = sb("sel", [P, 4, E], F32, pc)
            wsum = sb("wsum", [P, 4], F32, pc)
            rws = sb("rws", [P, 4], F32, pc)
            wts = sb("wts", [P, 2, 4, E], F32, pc)
            selv = sb("selv", [P, 2, 2, E], F32, pc)
            selT = sb("selT", [P, T // 2], F32, pc)
            cand = sb("cand", [P, SLOTS], F32, pc)
            both = sb("both", [E, 2 * SLOTS], F32, pc)
            topv = sb("topv", [E, SLOTS], F32, pc)
            tvc = sb("tvc", [SLOTS, E], F32, pc)
            emp = sb("emp", [SLOTS, E], F32, pc)
            tok = sb("tok", [SLOTS, E], F32, pc)

            with ExitStack() as pp:
                psT = ps("psT", [P, CH], pp)
                psL = ps("psL", [P, CH], pp)
                psV = ps("psV", [P, CH], pp)
                psQ = ps("psQ", [P, 4, CH], pp)
                psN = ps("psN", [P, CH], pp)
                names = ("ld_x ld_w ld_c consts_cast stat seps lnv rstd_ready zeroed zero_out scl xn_ready "
                         "xT_ps xT_ready lg_ps q_ps k_ps v_ps v_out turned cast resid n_ps n_ready "
                         "nmax_ready pexp routing selT_ps selT_ready st_xn0 st_xn1 st_xT0 st_xT1 st_parts0 st_parts1 st_nrm0 st_nrm1 st_w0 st_w1 dve_passed sp_passed").split()
                s = {n: sem(n, pp) for n in names}
                block = pp.enter_context(nc.Block())
                XG = 4
                xv = x.rearrange("(n p) d -> p n d", p=P)

                @block.sync
                def _(sp):
                    for g in range(XG):
                        n = TILES // XG
                        sp.dma_start(x_all[:, g * n:(g + 1) * n, :], xv[:, g * n:(g + 1) * n, :]).then_inc(s["ld_x"], 16)
                    sp.wait_ge(s["zeroed"], 1)
                    sp.dma_start(rows[T:T + DUMMY, :], zero[0:DUMMY, 0:ROW]).then_inc(s["zero_out"], 16)
                    step = 13
                    for r in range(0, T + DUMMY, step * P):
                        k = min(step, (T + DUMMY - r) // P)
                        if k:
                            sp.dma_start(routed[r:r + k * P, :].rearrange("(p n) d -> p (n d)", p=P),
                                         zero[:, 0:k * D]).then_inc(s["zero_out"], 16)
                    done = (T + DUMMY) // P * P
                    sp.dma_start(routed[done:T + DUMMY, :], zero[0:T + DUMMY - done, 0:D]).then_inc(s["zero_out"], 16)
                    nz = 2 + -(-(done // P) // step)

                    def chunk(b, hf):
                        g = b * 2 + hf
                        sp.wait_ge(s["xn_ready"], g * 4 + 4)
                        sp.dma_start(rows[bass.ds(g * CH, CH), 0:D].rearrange("(n p) d -> p n d", p=P),
                                     xn[:, hf]).then_inc(s["st_xn%d" % hf], 16)
                        wait_apart(sp, s["xT_ready"], g + 1, s["sp_passed"])
                        sp.dma_start(xT_d[:, bass.ds(g * CH, CH)], xT[:, hf]).then_inc(s["st_xT%d" % hf], 16)
                        sp.wait_ge(s["resid"], g * 6 + 4)
                        for w in range(2):
                            for gp in range(2):
                                for part in range(NPART):
                                    dst = qk_parts[bass.ds(b * 2 + gp, 1), w, :, part * HD:(part + 1) * HD,
                                                   hf * CH:(hf + 1) * CH]
                                    sp.dma_start(dst.rearrange("o h d s -> (o h) d s"),
                                                 parts[64 * gp:64 * gp + 64, hf, w, part, :]).then_inc(s["st_parts%d" % hf], 16)
                        sp.wait_ge(s["routing"], g * ROUTE + ROUTE)
                        sp.dma_start(rows[bass.ds(g * CH, CH), D:ROW].rearrange("(n p) d -> p n d", p=P),
                                     wts[:, hf]).then_inc(s["st_w%d" % hf], 16)
                        sp.wait_ge(s["resid"], g * 6 + 6)
                        for w in range(2):
                            for gp in range(2):
                                dst = nrm_parts[bass.ds(b * 2 + gp, 1), w, :, :, hf * CH:(hf + 1) * CH]
                                sp.dma_start(dst.rearrange("o h a s -> (o h) a s"),
                                             nparts[32 * w + 8 * gp:32 * w + 8 * gp + 8, hf]).then_inc(s["st_nrm%d" % hf], 16)

                    with sp.Fori(0, B) as b:
                        for hf in range(2):
                            chunk(b, hf)
                    sp.wait_ge(s["zero_out"], 16 * nz)
                    for hf in range(2):
                        for name, dmas in (("xn", 1), ("xT", 1), ("parts", 12), ("w", 1), ("nrm", 4)):
                            sp.wait_ge(s["st_%s%d" % (name, hf)], 16 * B * dmas)

                @block.gpsimd
                def _(pool):
                    nc.gpsimd.memset(zero[:], 0.0).then_inc(s["zeroed"], 1)
                    pool.wait_ge(s["zeroed"], 1)
                    nc.gpsimd.memset(q_d[64:P], 1.0).then_inc(s["zeroed"], 1)
                    pool.wait_ge(s["zeroed"], 2)
                    nc.gpsimd.memset(q_s[64:P], 0.0).then_inc(s["zeroed"], 1)
                    pool.wait_ge(s["zeroed"], 3)
                    nc.gpsimd.memset(k_t[64:P], 0.0).then_inc(s["zeroed"], 1)
                    pool.wait_ge(s["zeroed"], 4)
                    nc.gpsimd.memset(k_t[NORM_Q:NORM_Q + NPART], 1.0).then_inc(s["zeroed"], 1)

                    pool.wait_ge(s["zeroed"], 5)

                    def chunk(b, hf):
                        g = b * 2 + hf
                        for w in range(2):
                            pool.wait_ge(s["cast"], g * 8 + 3 * w + 1)
                            nc.gpsimd.tensor_tensor(res[:, w], qf[:, w], parts[:, hf, w, 0, :],
                                                    ALU.subtract).then_inc(s["resid"], 1)
                            pool.wait_ge(s["cast"], g * 8 + 3 * w + 3)
                            nc.gpsimd.tensor_tensor(parts[:, hf, w, 2, :], res[:, w], parts[:, hf, w, 1, :],
                                                    ALU.subtract).then_inc(s["resid"], 1)
                        pool.wait_ge(s["cast"], g * 8 + 7)
                        nc.gpsimd.tensor_tensor(nres[:], nf[:], nparts[:, hf, 0, :], ALU.subtract).then_inc(s["resid"], 1)
                        pool.wait_ge(s["cast"], g * 8 + 8)
                        nc.gpsimd.tensor_tensor(nparts[:, hf, 2, :], nres[:], nparts[:, hf, 1, :],
                                                ALU.subtract).then_inc(s["resid"], 1)

                    with pool.Fori(0, B) as b:
                        for hf in range(2):
                            chunk(b, hf)

                @block.scalar
                def _(act):
                    for dst, src in ((w_q, wq), (w_qs, wqs), (w_k, wk), (w_ks, wks), (w_v, wv), (w_r, rwt), (al, alpha)):
                        act.dma_start(dst[:], src).then_inc(s["ld_w"], 16)
                    act.dma_start(cst[:], consts).then_inc(s["ld_c"], 16)
                    act.dma_start(tabs[:], rope).then_inc(s["ld_c"], 16)
                    nc.scalar.preload_act_table_set(ACT_SET)
                    act.wait_ge(s["ld_w"], 16 * 7)
                    nc.scalar.activation(scale[:], al[:], ACT.Exp,
                                         scale=float(np.log(np.sqrt(np.float32(HD)) / np.log(np.float32(1 + HD))))
                                         ).then_inc(s["scl"], 1)
                    act.wait_ge(s["seps"], 1)
                    nc.scalar.activation(rstd[:], rstd[:], ACT.Ln).then_inc(s["lnv"], 1)
                    act.wait_ge(s["lnv"], 1)
                    nc.scalar.activation(rstd[:], rstd[:], ACT.Exp, scale=-0.5).then_inc(s["rstd_ready"], 1)

                    def chunk(b, hf, first):
                        g = b * 2 + hf
                        if not first:
                            act.wait_ge(s["st_xT%d" % hf], 16 * b)
                        act.wait_ge(s["xT_ps"], g + 1)
                        nc.scalar.activation(xT[:, hf], psT[:], ACT.Copy).then_inc(s["xT_ready"], 1)
                        act.wait_ge(s["nmax_ready"], g + 1)
                        for i in range(4):
                            nc.scalar.activation(pe_[:, i, :], psL[:, i * E:(i + 1) * E], ACT.Exp,
                                                 bias=nmax[:, i:i + 1]).then_inc(s["pexp"], 1)
                        for w in range(2):
                            if not first:
                                act.wait_ge(s["st_parts%d" % hf], 16 * 12 * b)
                            act.wait_ge(s["turned"], g * 6 + 3 * w + 3)
                            nc.scalar.activation(parts[:, hf, w, 0, :], qf[:, w], ACT.Copy).then_inc(s["cast"], 1)
                            nc.scalar.activation(sq[:, w], qf[:, w], ACT.Square).then_inc(s["cast"], 1)
                            act.wait_ge(s["resid"], g * 6 + 2 * w + 1)
                            nc.scalar.activation(parts[:, hf, w, 1, :], res[:, w], ACT.Copy).then_inc(s["cast"], 1)
                            if w == 0:
                                act.wait_ge(s["v_ps"], g + 1)
                                dst = v_all[:, bass.ds(b * 2, 2), 4 * hf:4 * hf + 4, :]
                                nc.scalar.activation(dst, psV[:].rearrange("p (i g c) -> p g i c", i=4, g=2),
                                                     ACT.Copy).then_inc(s["v_out"], 1)
                        if not first:
                            act.wait_ge(s["st_nrm%d" % hf], 16 * 4 * b)
                        act.wait_ge(s["n_ready"], g + 1)
                        nc.scalar.activation(nparts[:, hf, 0, :], nf[:], ACT.Copy).then_inc(s["cast"], 1)
                        act.wait_ge(s["resid"], g * 6 + 5)
                        nc.scalar.activation(nparts[:, hf, 1, :], nres[:], ACT.Copy).then_inc(s["cast"], 1)
                        act.wait_ge(s["selT_ps"], g + 1)
                        nc.scalar.activation(selT[:, bass.ds(g * 256, 256)], psL[:, 256:512], ACT.Copy).then_inc(s["selT_ready"], 1)

                    for hf in range(2):
                        chunk(0, hf, True)
                    with act.Fori(1, B) as b:
                        for hf in range(2):
                            chunk(b, hf, False)

                @block.tensor
                def _(pe):
                    pe.wait_ge(s["ld_w"], 16 * 7)
                    pe.wait_ge(s["ld_c"], 32)

                    def chunk(b, hf, first):
                        g = b * 2 + hf
                        pe.wait_ge(s["xn_ready"], g * 4 + 4)
                        if not first:
                            pe.wait_ge(s["xT_ready"], g)
                        for i in range(4):
                            last = nc.tensor.transpose(psT[:, i * P:(i + 1) * P], xn[:, hf, i, :], cst[:, 0:P])
                        last.then_inc(s["xT_ps"], 1)
                        pe.wait_ge(s["xT_ready"], g + 1)
                        if not first:
                            pe.wait_ge(s["selT_ready"], g)
                        for i in range(4):
                            last = nc.tensor.matmul(psL[:, i * E:(i + 1) * E], xT[:, hf, i * P:(i + 1) * P], w_r[:],
                                                    start=True, stop=True)
                        last.then_inc(s["lg_ps"], 1)
                        for w, (wa, wb) in enumerate(((w_q, w_qs), (w_k, w_ks))):
                            if not first:
                                pe.wait_ge(s["turned"], (g - 1) * 6 + 3 * w + 2)
                            nc.tensor.matmul(psQ[:, 2 * w, :], wa[:], xT[:, hf], start=True, stop=True)
                            nc.tensor.matmul(psQ[:, 2 * w + 1, :], wb[:], xT[:, hf], start=True, stop=True)\
                                .then_inc(s["k_ps" if w else "q_ps"], 1)
                        if not first:
                            pe.wait_ge(s["v_out"], g)
                        for i in range(4):
                            last = nc.tensor.matmul(psV[:, i * P:(i + 1) * P], xT[:, hf, i * P:(i + 1) * P], w_v[:],
                                                    start=True, stop=True)
                        last.then_inc(s["v_ps"], 1)
                        pe.wait_ge(s["cast"], g * 8 + 5)
                        if not first:
                            pe.wait_ge(s["n_ready"], g)
                        for w in range(2):
                            last = nc.tensor.matmul(psN[32 * w:32 * w + 32, :], cst[:, C_NB:C_NB + 32], sq[:, w],
                                                    start=True, stop=True)
                        last.then_inc(s["n_ps"], 1)
                        pe.wait_ge(s["routing"], g * ROUTE + ROUTE)
                        for j in range(2):
                            last = nc.tensor.transpose(psL[:, 256 + j * P:256 + (j + 1) * P],
                                                       selv[:, j].rearrange("p a e -> p (a e)"), cst[:, 0:P])
                        last.then_inc(s["selT_ps"], 1)

                    chunk(0, 0, True)
                    chunk(0, 1, False)
                    with pe.Fori(1, B) as b:
                        for hf in range(2):
                            chunk(b, hf, False)

                @block.vector
                def _(dve):
                    dve.wait_ge(s["ld_c"], 32)
                    for dst, c0 in ((identb, 0), (mask_d, C_MD), (mask_t, C_MT), (ident, 0)):
                        nc.vector.tensor_copy(dst[:], cst[:, c0:c0 + P]).then_inc(s["consts_cast"], 1)
                    for n in range(TILES):
                        if n % (TILES // XG) == 0:
                            dve.wait_ge(s["ld_x"], 16 * XG)
                        nc.vector.bn_stats(st6[:, n, :], x_all[:, n, :]).then_inc(s["stat"], 1)
                    for n in range(TILES):
                        if n == 0:
                            dve.wait_ge(s["stat"], TILES)
                        nc.vector.bn_aggr(mv[:, n, :], st6[:, n, :]).then_inc(s["stat"], 1)
                    dve.wait_ge(s["stat"], 2 * TILES)
                    nc.vector.tensor_scalar(rstd[:], mv[:, :, 1], LN_EPS, None, ALU.add).then_inc(s["seps"], 1)
                    dve.wait_ge(s["rstd_ready"], 1)

                    def chunk(b, hf, first, second):
                        g = b * 2 + hf
                        if not first:
                            dve.wait_ge(s["st_xn%d" % hf], 16 * b)
                            dve.wait_ge(s["xT_ps"], g - 1)
                        for i in range(4):
                            n = g * 4 + i
                            nc.vector.tensor_scalar(xn[:, hf, i, :], x_all[:, bass.ds(n, 1), :].rearrange("p o d -> p (o d)"),
                                                    mv[:, bass.ds(n, 1), 0], rstd[:, bass.ds(n, 1)],
                                                    ALU.subtract, ALU.mult).then_inc(s["xn_ready"], 1)
                        dve.wait_ge(s["lg_ps"], g + 1)
                        if not (first and not second):
                            dve.wait_ge(s["pexp"], g * 4)
                        nc.vector.tensor_reduce(nmax[:], psL[:, 0:256].rearrange("p (i e) -> p i e", i=4), AXX, ALU.max,
                                                negate=True).then_inc(s["nmax_ready"], 1)
                        n_turn = 0
                        for w in range(2):
                            dve.wait_ge(s["k_ps" if w else "q_ps"], g + 1)
                            nc.vector.tensor_tensor(ra[:, w], psQ[:, 2 * w, :], tabs[:, 0, hf * CH:(hf + 1) * CH],
                                                    ALU.mult).then_inc(s["turned"], 1)
                            nc.vector.tensor_tensor(rb[:, w], psQ[:, 2 * w + 1, :], tabs[:, 1, hf * CH:(hf + 1) * CH],
                                                    ALU.mult).then_inc(s["turned"], 1)
                            n_turn += 2
                            dve.wait_ge(s["turned"], g * 6 + 3 * w + 2)
                            if not (first and not second):
                                dve.wait_ge(s["cast"], (g - 1) * 8 + 3 * w + 2)
                                dve.wait_ge(s["resid"], (g - 1) * 6 + 2 * w + 1)
                            nc.vector.tensor_tensor(qf[:, w], ra[:, w], rb[:, w], ALU.add).then_inc(s["turned"], 1)
                        count = [0]

                        def mark(ins):
                            ins.then_inc(s["routing"], 1)
                            count[0] += 1

                        def settled():
                            wait_apart(dve, s["routing"], g * ROUTE + count[0], s["dve_passed"])
                        wait_apart(dve, s["pexp"], g * 4 + 4, s["dve_passed"])
                        for i in range(4):
                            mark(nc.vector.max(top8[:, i, :], pe_[:, i, :]))
                        settled()
                        for i in range(4):
                            mark(nc.vector.match_replace(mr[:, i, :], top8[:, i, :], pe_[:, i, :], -1.0))
                        mark(nc.vector.reduce_sum(wsum[:], top8[:], AXX))
                        settled()
                        mark(nc.vector.tensor_scalar(sel[:], mr[:], 0.0, None, ALU.is_lt))
                        mark(nc.vector.reciprocal(rws[:], wsum[:]))
                        settled()
                        if not (first and not second):
                            dve.wait_ge(s["selT_ps"], g)
                        for i in range(4):
                            mark(nc.vector.tensor_scalar(selv[:, i % 2, i // 2, :], sel[:, i, :],
                                                         cst[:, bass.ds(C_TV + g * 4 + i, 1)], None, ALU.mult))
                        if not first:
                            dve.wait_ge(s["st_w%d" % hf], 16 * b)
                        for i in range(4):
                            mark(nc.vector.scalar_tensor_tensor(wts[:, hf, i, :], pe_[:, i, :], rws[:, i:i + 1], sel[:, i, :],
                                                                ALU.mult, ALU.mult))
                        assert count[0] == ROUTE
                        dve.wait_ge(s["n_ps"], g + 1)
                        if not (first and not second):
                            dve.wait_ge(s["resid"], (g - 1) * 6 + 6)
                        nc.vector.tensor_scalar(nf[:], psN[0:64, :], -0.25 * ATT_EPS, None, ALU.add).then_inc(s["n_ready"], 1)

                    chunk(0, 0, True, False)
                    chunk(0, 1, True, True)
                    with dve.Fori(1, B) as b:
                        for hf in range(2):
                            chunk(b, hf, False, False)

            with ExitStack() as pp:
                psX = ps("psX", [P, CH], pp)
                s = {n: sem(n, pp) for n in "found tv_ps idx_ready idx_cast".split()}
                block = pp.enter_context(nc.Block())

                @block.vector
                def _(dve):
                    n = 0

                    def done(ins):
                        nonlocal n
                        n += 1
                        ins.then_inc(s["found"], 1)
                        dve.wait_ge(s["found"], n)

                    for r in range(SLOTS // 8):
                        m = cand[:, 8 * r:8 * r + 8]
                        done(nc.vector.max(m, selT[:]))
                        done(nc.vector.match_replace(selT[:], m, selT[:], 0.0))
                    done(nc.vector.tensor_copy(both[:, 0:SLOTS], cand[0:E, :]))
                    done(nc.vector.tensor_copy(both[:, SLOTS:2 * SLOTS], cand[E:P, :]))
                    for r in range(SLOTS // 8):
                        m = topv[:, 8 * r:8 * r + 8]
                        done(nc.vector.max(m, both[:]))
                        done(nc.vector.match_replace(both[:], m, both[:], 0.0))
                    dve.wait_ge(s["tv_ps"], 1)
                    done(nc.vector.tensor_scalar(emp[:], psX[0:SLOTS, 0:E], 0.0, cst[0:SLOTS, C_SI:C_SI + 1],
                                                 ALU.is_equal, ALU.mult))
                    done(nc.vector.tensor_scalar(tok[:], psX[0:SLOTS, 0:E], -1.0, float(T), ALU.mult, ALU.add))
                    done(nc.vector.tensor_tensor(tok[:], tok[:], emp[:], ALU.add))
                    done(nc.vector.tensor_copy(idx64[:], tok[:]))
                    pairs = tok[:].rearrange("c (r o) -> c o r", o=2)
                    done(nc.vector.tensor_copy(idxp[0:SLOTS, :], pairs[:, 0, :]))
                    done(nc.vector.tensor_copy(idxp[SLOTS:P, :], pairs[:, 1, :]))

                @block.tensor
                def _(pe):
                    pe.wait_ge(s["found"], 2 * (SLOTS // 8) * 2 + 2)
                    nc.tensor.transpose(psX[0:SLOTS, 0:E], topv[:], cst[0:E, 0:E]).then_inc(s["tv_ps"], 1)

        shared = dict(ident=ident, identb=identb, q_d=q_d, q_s=q_s, k_t=k_t,
                      mask_d=mask_d, mask_t=mask_t, scale=scale, v_all=v_all, idx64=idx64,
                      idxp=idxp, qk_parts=qk_parts, nrm_parts=nrm_parts, rows=rows, routed=routed,
                      xT_d=xT_d, att_d=att_d)
        attend(nc, shared, wgu, wdn)
        output(nc, shared, x, wo, wsgu, wsdn, out)



def attend(nc, m, wgu, wdn):
    with ExitStack() as ctx:
        def sb(name, shape, dt=F32):
            return ctx.enter_context(nc.sbuf_tensor(name, shape, dt))

        def ps(name, shape):
            return ctx.enter_context(nc.psum_tensor(name, shape, F32))

        q_d, q_s, k_t = m["q_d"], m["q_s"], m["k_t"]
        v_aug = sb("v_aug", [P, 2, QT, GH, 32])
        r_buf = sb("r_buf", [P, 2, S])
        z_buf = sb("z_buf", [P, 4, S])
        m_buf = sb("m_buf", [P, 8, GH])
        p_buf = sb("p_buf", [P, 2, GH, S])
        o_t = sb("o_t", [P, 16, 32])
        o_rc = sb("o_rc", [P, 16])
        o_n = sb("o_n", [P, 2, CH])
        xg = sb("xg", [P, 2, ROW])
        xgT = sb("xgT", [P, P])
        w_gu = sb("w_gu", [P, 2, 2, 2 * F])
        w_dn = sb("w_dn", [F, 2, 2, D])
        h_a = sb("h_a", [P, F])
        h_b = sb("h_b", [P, F])
        hT = sb("hT", [F, P])
        ys = sb("ys", [SLOTS, 2, 2, D])
        gidx = sb("gidx", [P, 2, 1], I32)
        sidx = sb("sidx", [SLOTS, 2, 2], I32)

        ps_d = ps("ps_d", [P, S])
        ps_s = ps("ps_s", [P, S])
        ps_t = ps("ps_t", [P, S])
        ps_o = ps("ps_o", [P, CH])
        ps_m = ps("ps_m", [P, CH])

        names = ("ld0 ld1 d_ready s_ready ln_done r_ready z_done m_done u_ready t_ready p_done pv_done "
                 "o_turned o_step o_out o_stored0 o_stored1 v_loaded v_clear ld_w0 ld_w1 x_idx x_got0 x_got1 xT_ps xT_ok gu_ps "
                 "gu_exp h_step hT_ps hT_ok y_ps y_ok sc_idx scat dve_passed sp_passed pool_passed").split()
        s = {n: ctx.enter_context(nc.semaphore("b_" + n)) for n in names}
        block = ctx.enter_context(nc.Block())
        LOADS = 9 + 9 + 3 + 2
        PAIR_AT = NT // 4
        PV0, YPS0, YOK0, PD0 = 9, 2, 4, 1

        def seg(buf, step):
            i, heads, pitch = step
            return buf[:, 0:len(heads) * pitch].rearrange("p (c w) -> p c w", c=len(heads))[:, :, 0:P * (i + 1)]

        def unit_of(n):
            return 8 * (n // NS) + (QT - 1 - STEPS[n % NS][0])

        def trips(eng, lead, stages):
            def iteration(t, n, last):
                for ahead, stage in stages:
                    if n + ahead < NT:
                        stage(t, n + ahead)
                    elif not last:
                        stage(t + 1, n + ahead - NT)

            for n in range(-lead, 0):
                for ahead, stage in stages:
                    if n + ahead >= 0:
                        stage(0, n + ahead)
            with eng.Fori(0, TRIPS - 1) as t:
                for n in range(NT):
                    iteration(t, n, False)
            for n in range(NT):
                iteration(TRIPS - 1, n, True)

        @block.sync
        def _(sp):
            def load(t, par):
                ld = s["ld%d" % par]
                h0 = 4 * par
                src = m["qk_parts"][bass.ds(t, 1)].rearrange("o w h r s -> (o w) r h s")
                nrm = m["nrm_parts"][bass.ds(t, 1)].rearrange("o w h a s -> (o w) a h s")
                for a in range(NPART):
                    for b in range(NPART):
                        r = (a * NPART + b) * HD
                        qa = src[0, a * HD:(a + 1) * HD, h0:h0 + GH, :]
                        sp.dma_start(q_d[r:r + HD, par], qa).then_inc(ld, 16)
                        sp.dma_start(q_s[r:r + HD, par], qa).then_inc(ld, 16)
                    r = a * NPART * HD
                    sp.dma_start(k_t[r:r + NPART * HD, par], src[1, :, h0:h0 + GH, :]).then_inc(ld, 16)
                sp.dma_start(q_d[NORM_Q:NORM_Q + NPART, par], nrm[0, :, h0:h0 + GH, :]).then_inc(ld, 16)
                sp.dma_start(k_t[NORM_K:NORM_K + NPART, par], nrm[1, :, h0:h0 + GH, :]).then_inc(ld, 16)

            def weights(t, p):
                ld = s["ld_w%d" % (p % 2)]
                wait_apart(sp, s["y_ps"], YPS0 + t * 4 + p - 1, s["sp_passed"])
                e0 = t * 8 + 2 * p
                sp.dma_start(w_gu[:, p % 2], wgu[bass.ds(e0, 2)].rearrange("e d f -> d e f")).then_inc(ld, 16)
                sp.dma_start(w_dn[:, p % 2], wdn[bass.ds(e0, 2)].rearrange("e f d -> f e d")).then_inc(ld, 16)

            load(0, 0)
            load(0, 1)
            weights(0, 0)
            weights(0, 1)

            def store(t, k):
                par, hh = k // 2, k % 2
                wait_apart(sp, s["o_out"], t * 4 + k + 2, s["sp_passed"])
                for c in range(GH):
                    sp.dma_start(m["att_d"][bass.ds(t, 1), par, c * HD:(c + 1) * HD, CH * (1 - hh):CH * (2 - hh)]
                                 .rearrange("o r q -> (o r) q"), o_n[32 * c:32 * c + HD, hh, :]).then_inc(s["o_stored%d" % hh], 16)

            with sp.Fori(0, TRIPS - 1) as t:
                weights(t, 2)
                store(t, 0)
                sp.wait_ge(s["s_ready"], t * NT + NS)
                load(t + 1, 0)
                weights(t, 3)
                store(t, 1)
                weights(t + 1, 0)
                store(t, 2)
                sp.wait_ge(s["s_ready"], t * NT + NT)
                load(t + 1, 1)
                weights(t + 1, 1)
                store(t, 3)
            weights(TRIPS - 1, 2)
            store(TRIPS - 1, 0)
            weights(TRIPS - 1, 3)
            for k in range(1, 4):
                store(TRIPS - 1, k)
            for hh in range(2):
                sp.wait_ge(s["o_stored%d" % hh], 16 * 4 * (1 + 2 * TRIPS))

        @block.gpsimd
        def _(pool):
            for par in range(2):
                nc.gpsimd.memset(v_aug[:, par], 0.0).then_inc(s["v_clear"], 1)
            pool.wait_ge(s["v_clear"], 2)
            for par in range(2):
                nc.gpsimd.memset(v_aug[:, par, :, :, HD], 1.0).then_inc(s["v_clear"], 1)

            def values(t, par):
                pool.wait_ge(s["pv_done"], PV0 + t * 16 + 8 * par - 8)
                src = m["v_all"][:, bass.ds(t, 1), :, 32 * par:32 * par + 32].rearrange("p o j (c d) -> p (o j) c d", c=GH)
                nc.gpsimd.tensor_copy(v_aug[:, par, :, :, 0:HD], src).then_inc(s["v_loaded"], 1)

            def gather(t, p):
                g = t * 4 + p
                pool.wait_ge(s["y_ok"], YOK0 + 2 * g - 2)
                nc.gpsimd.tensor_copy(gidx[:, p % 2], m["idxp"][:, bass.ds(g, 1)]).then_inc(s["x_idx"], 1)
                wait_apart(pool, s["x_idx"], g + 1, s["pool_passed"])
                nc.gpsimd.indirect_dma_start(xg[:, p % 2], None, m["rows"], bass.IndirectOffsetOnAxis(gidx[:, p % 2], 0)
                                             ).then_inc(s["x_got%d" % (p % 2)], 16)

            def added(t, p, e):
                wait_apart(pool, s["scat"], 16 * (2 * (t * 4 + p) + e + 1), s["pool_passed"])

            def scatter(t, p, e):
                g = t * 4 + p
                if e == 0:
                    nc.gpsimd.tensor_copy(sidx[:, p % 2], m["idx64"][:, bass.ds(2 * g, 2)]).then_inc(s["sc_idx"], 1)
                    wait_apart(pool, s["sc_idx"], g + 1, s["pool_passed"])
                    wait_apart(pool, s["y_ok"], YOK0 + g * 2 + 2, s["pool_passed"])
                else:
                    added(t, p, 0)
                nc.gpsimd.indirect_dma_start(m["routed"], bass.IndirectOffsetOnAxis(sidx[:, p % 2, e:e + 1], 0),
                                             ys[:, p % 2, e, :], None, compute_op=ALU.add).then_inc(s["scat"], 16)

            def shift(t, n):
                g = t * NT + n
                if n % NS == 0:
                    values(t, n // NS)
                pool.wait_ge(s["m_done"], g + 1)
                step = STEPS[n % NS]
                k = len(step[1])
                z = seg(z_buf[:, n % 4], step)
                nc.gpsimd.tensor_tensor(z, z, m_buf[:, n % 8, 0:k].unsqueeze(2).to_broadcast([P, k, P * (step[0] + 1)]),
                                        ALU.subtract).then_inc(s["u_ready"], 1)
                q, r = n % PAIR_AT, n // PAIR_AT
                if q == 0:
                    gather(t, r)
                if q == 8:
                    scatter(t, r, 0)
                if q == 9:
                    scatter(t, r, 1)
                if q == 10:
                    added(t, r, 1)

            trips(pool, 0, ((0, shift),))

        @block.scalar
        def _(act):
            nc.scalar.preload_act_table_set(ACT_SET)

            act.sem_inc(s["p_done"], PD0)

            def log(t, n):
                g = t * NT + n
                step = STEPS[n % NS]
                ge(act, s["z_done"], g - 1)
                act.wait_ge(s["d_ready"], g + 1)
                nc.scalar.activation(seg(r_buf[:, n % 2], step), seg(ps_d, step), ACT.Ln, scale=-2.0).then_inc(s["ln_done"], 1)

            def root(t, n):
                g = t * NT + n
                step = STEPS[n % NS]
                r = seg(r_buf[:, n % 2], step)
                act.wait_ge(s["ln_done"], g + 1)
                nc.scalar.activation(r, r, ACT.Exp, scale=-0.5).then_inc(s["r_ready"], 1)

            def probs(t, n):
                g = t * NT + n
                step = STEPS[n % NS]
                i, heads, _ = step
                u = unit_of(n)
                act.wait_ge(s["t_ready"], g + 1)
                act.wait_ge(s["pv_done"], PV0 + t * 16 + u - 1)
                nc.scalar.activation(p_buf[:, u % 2, heads[0]:heads[-1] + 1, 0:P * (i + 1)], seg(ps_t, step),
                                     ACT.Exp).then_inc(s["p_done"], 1)

            def experts(t, n):
                if n % PAIR_AT == 3:
                    g = t * 4 + n // PAIR_AT
                    act.wait_ge(s["gu_ps"], g + 1)
                    nc.scalar.activation(h_a[:], ps_m[:, 128:128 + F], ACT.Exp, scale=-1.0).then_inc(s["gu_exp"], 1)

            trips(act, LEAD, ((LEAD, log), (0, probs), (LEAD, root), (0, experts)))

        @block.tensor
        def _(pe):
            pe.sem_inc(s["pv_done"], PV0)
            pe.sem_inc(s["y_ps"], YPS0)

            def products(out, qs, t, n):
                g = t * NT + n
                par, (i, heads, pitch) = n // NS, STEPS[n % NS]
                w = P * (i + 1)
                for a, c in enumerate(heads):
                    for k0 in range(0, w, CH):
                        k1 = min(w, k0 + CH)
                        diag = out is ps_d and k1 == w
                        last = nc.tensor.matmul(out[:, a * pitch + k0:a * pitch + k1], qs[:, par, c, i * P:(i + 1) * P],
                                                k_t[:, par, c, k0:k1], start=True, stop=not diag)
                        if diag:
                            last = nc.tensor.matmul(out[:, a * pitch + w - P:a * pitch + w], m["identb"][:], m["mask_d"][:],
                                                    start=False, stop=True)
                return last

            def distances(t, n):
                if n % NS == 0:
                    pe.wait_ge(s["ld%d" % (n // NS)], (t + 1) * 16 * LOADS)
                ge(pe, s["ln_done"], t * NT + n)
                products(ps_d, q_d, t, n).then_inc(s["d_ready"], 1)

            def scores(t, n):
                ge(pe, s["z_done"], t * NT + n)
                products(ps_s, q_s, t, n).then_inc(s["s_ready"], 1)

            def values(t, n):
                par = n // NS
                for i, j0, j1 in VALUES[n % NS]:
                    u = 8 * par + QT - 1 - i
                    if j0 == 0:
                        end = par * NS + max(a for a in range(NS) if STEPS[a][0] == i)
                        pe.wait_ge(s["p_done"], PD0 + t * NT + end + 1)
                        if i == QT - 1:
                            pe.wait_ge(s["v_loaded"], t * 2 + par + 1)
                        if i % 4 == 3:
                            pe.wait_ge(s["o_turned"], t * 4 + u // 4 + 1)
                    for j in range(j0, j1):
                        for c in range(GH):
                            last = nc.tensor.matmul(ps_o[32 * c:32 * c + 32, (i % 4) * P:(i % 4 + 1) * P],
                                                    v_aug[:, par, j, c, :], p_buf[:, u % 2, c, j * P:(j + 1) * P],
                                                    start=j == 0, stop=j == i)
                    if j1 == i + 1:
                        last.then_inc(s["pv_done"], 1)

            def turn(t, n):
                g = t * NT + n
                i, heads, pitch = STEPS[n % NS]
                pe.wait_ge(s["u_ready"], g + 1)
                pe.wait_ge(s["p_done"], PD0 + g)
                for a in range(len(heads)):
                    for j in range(i + 1):
                        o = a * pitch + j * P
                        diag = j == i
                        last = nc.tensor.matmul(ps_t[:, o:o + P], z_buf[:, n % 4, o:o + P], m["ident"][:], start=True,
                                                stop=not diag, is_transpose=True)
                        if diag:
                            last = nc.tensor.matmul(ps_t[:, o:o + P], m["identb"][:], m["mask_t"][:], start=False, stop=True)
                last.then_inc(s["t_ready"], 1)

            def experts(t, n):
                q, p = n % PAIR_AT, n // PAIR_AT
                g = t * 4 + p
                if q == 2:
                    pe.wait_ge(s["x_got%d" % (p % 2)], 16 * (t * 2 + p // 2 + 1))
                    pe.wait_ge(s["y_ok"], YOK0 + 2 * g)
                    nc.tensor.transpose(ps_m[:, 0:P], xg[:, p % 2, 0:D], m["ident"][:]).then_inc(s["xT_ps"], 1)
                if q == 3:
                    pe.wait_ge(s["ld_w%d" % (p % 2)], 32 * (t * 2 + p // 2 + 1))
                    pe.wait_ge(s["xT_ok"], g + 1)
                    for e in range(2):
                        last = nc.tensor.matmul(ps_m[SLOTS * e:SLOTS * (e + 1), 128:128 + 2 * F],
                                                xgT[:, SLOTS * e:SLOTS * (e + 1)], w_gu[:, p % 2, e, :], start=True, stop=True)
                    last.then_inc(s["gu_ps"], 1)
                if q == 5:
                    pe.wait_ge(s["h_step"], g * 4 + 4)
                    nc.tensor.transpose(ps_m[0:F, 320:448], h_a[:], m["ident"][:]).then_inc(s["hT_ps"], 1)
                if q == 6:
                    pe.wait_ge(s["hT_ok"], g + 1)
                    for e in range(2):
                        last = nc.tensor.matmul(ps_m[SLOTS * e:SLOTS * (e + 1), 0:D], hT[:, SLOTS * e:SLOTS * (e + 1)],
                                                w_dn[:, p % 2, e, :], start=True, stop=True)
                    last.then_inc(s["y_ps"], 1)

            trips(pe, LEAD, ((LEAD, distances), (LEAD - 1, scores), (0, turn), (0, experts), (0, values)))

        @block.vector
        def _(dve):
            dve.sem_inc(s["o_turned"], 1)
            dve.sem_inc(s["o_out"], 1)
            dve.sem_inc(s["y_ok"], YOK0)
            for hh in range(2):
                dve.sem_inc(s["o_stored%d" % hh], 16 * 4)

            def ratios(t, n):
                g = t * NT + n
                step = STEPS[n % NS]
                dve.wait_ge(s["r_ready"], g + 1)
                dve.wait_ge(s["s_ready"], g + 1)
                nc.vector.tensor_tensor(seg(z_buf[:, n % 4], step), seg(ps_s, step), seg(r_buf[:, n % 2], step),
                                        ALU.mult).then_inc(s["z_done"], 1)

            def squares(t, n):
                g = t * NT + n
                step = STEPS[n % NS]
                wait_apart(dve, s["z_done"], g + 1, s["dve_passed"])
                z = seg(z_buf[:, n % 4], step)
                for a in range(len(step[1])):
                    last = nc.vector.tensor_tensor_reduce(out=z[:, a], in0=z[:, a], in1=z[:, a], scale=m["scale"][:], scalar=0.0,
                                                          op0=ALU.mult, op1=ALU.max, accum_out=m_buf[:, n % 8, a:a + 1])
                last.then_inc(s["m_done"], 1)

            def divide(t, n):
                par, hh = n // NS, HALF_END.index(n % NS)
                half = t * 4 + 2 * par + hh
                dve.wait_ge(s["pv_done"], PV0 + t * 16 + 8 * par + 4 * hh + 4)
                dve.wait_ge(s["o_out"], half + 1)
                ov = o_t[:].rearrange("p f r -> p (f r)")
                nc.vector.transpose(ov, ps_o[:]).then_inc(s["o_turned"], 1)
                dve.wait_ge(s["o_turned"], half + 2)
                nc.vector.reciprocal(o_rc[:], o_t[:, :, HD]).then_inc(s["o_step"], 1)
                dve.wait_ge(s["o_step"], half * 2 + 1)
                nc.vector.tensor_tensor(o_t[:, :, 0:HD], o_t[:, :, 0:HD], o_rc[:].unsqueeze(2).to_broadcast([P, 16, HD]),
                                        ALU.mult).then_inc(s["o_step"], 1)
                dve.wait_ge(s["o_step"], half * 2 + 2)
                dve.wait_ge(s["o_stored%d" % hh], 16 * 4 * (2 * t + par + 1))
                nc.vector.transpose(o_n[:, hh], ov).then_inc(s["o_out"], 1)

            def experts(t, n):
                q, p = n % PAIR_AT, n // PAIR_AT
                g = t * 4 + p
                if q == 2:
                    dve.wait_ge(s["xT_ps"], g + 1)
                    nc.vector.tensor_copy(xgT[:], ps_m[:, 0:P]).then_inc(s["xT_ok"], 1)
                if q == 4:
                    dve.wait_ge(s["gu_exp"], g + 1)
                    nc.vector.tensor_scalar(h_b[:], h_a[:], 1.0, None, ALU.add).then_inc(s["h_step"], 1)
                    dve.wait_ge(s["h_step"], g * 4 + 1)
                    nc.vector.reciprocal(h_a[:], h_b[:]).then_inc(s["h_step"], 1)
                    dve.wait_ge(s["h_step"], g * 4 + 2)
                    nc.vector.tensor_tensor(h_b[:], ps_m[:, 128:128 + F], h_a[:], ALU.mult).then_inc(s["h_step"], 1)
                    dve.wait_ge(s["h_step"], g * 4 + 3)
                    nc.vector.tensor_tensor(h_a[:], ps_m[:, 128 + F:128 + 2 * F], h_b[:], ALU.mult).then_inc(s["h_step"], 1)
                if q == 5:
                    dve.wait_ge(s["hT_ps"], g + 1)
                    nc.vector.tensor_copy(hT[:], ps_m[0:F, 320:448]).then_inc(s["hT_ok"], 1)
                if q == 6:
                    dve.wait_ge(s["y_ps"], YPS0 + g + 1)
                    for e in range(2):
                        a, b = SLOTS * e, SLOTS * (e + 1)
                        last = nc.vector.tensor_scalar(ys[:, p % 2, e, :], ps_m[a:b, 0:D],
                                                       xg[a:b, p % 2, bass.ds(D + 2 * g + e, 1)], None, ALU.mult)
                        last.then_inc(s["y_ok"], 1)

            def rest(t, n):
                if n % NS in HALF_END:
                    divide(t, n)
                experts(t, n)

            trips(dve, LEAD - 1, ((LEAD - 1, ratios), (LEAD - 1, squares), (0, rest)))


def output(nc, m, x, wo, wsgu, wsdn, out):
    with ExitStack() as ctx:
        def sb(name, shape, dt=F32):
            return ctx.enter_context(nc.sbuf_tensor(name, shape, dt))

        def ps(name, shape):
            return ctx.enter_context(nc.psum_tensor(name, shape, F32))

        w_o = sb("w_o", [P, D])
        w_sgu = sb("w_sgu", [P, 2 * F])
        w_sdn = sb("w_sdn", [F, D])
        a_t = sb("a_t", [P, 2, CH])
        x_t = sb("x_t", [P, 2, CH])
        x_r = sb("x_r", [P, 2, 4, D])
        r_r = sb("r_r", [P, 2, 4, D])
        sg = sb("sg", [F, 2, CH])
        sg1 = sb("sg1", [F, 2, CH])
        h_t = sb("h_t", [F, 2, CH])
        acc = sb("acc", [P, 2, 4, D])
        res = sb("res_out", [P, 2, 4, D])
        psg = ps("psg", [P, 2, CH])
        psu = ps("psu", [P, 2, CH])
        psy = ps("psy", [P, 2, CH])
        s = {n: ctx.enter_context(nc.semaphore("c_" + n)) for n in
             "ld_w ld0 ld1 gu ex hs y sum stored0 stored1".split()}
        block = ctx.enter_context(nc.Block())

        @block.sync
        def _(sp):
            for dst, src in ((w_o, wo), (w_sgu, wsgu), (w_sdn, wsdn)):
                sp.dma_start(dst[:], src).then_inc(s["ld_w"], 16)

            def load(b, hf, first=False):
                g = b * 2 + hf
                ld = s["ld%d" % hf]
                if not first:
                    sp.wait_ge(s["sum"], 2 * g - 2)
                src = m["att_d"][bass.ds(2 * b, 2), :, :, hf * CH:(hf + 1) * CH].rearrange("g p r q -> (g p r) q")
                sp.dma_start(a_t[:, hf], src).then_inc(ld, 16)
                sp.dma_start(x_t[:, hf], m["xT_d"][:, bass.ds(g * CH, CH)]).then_inc(ld, 16)
                for dst, src in ((x_r, x), (r_r, m["routed"])):
                    sp.dma_start(dst[:, hf], src[bass.ds(g * CH, CH), :].rearrange("(n p) d -> p n d", p=P)).then_inc(ld, 16)

            for hf in range(2):
                load(0, hf, True)
            with sp.Fori(1, B) as b:
                for hf in range(2):
                    load(b, hf)

        @block.scalar
        def _(act):
            nc.scalar.preload_act_table_set(ACT_SET)
            with act.Fori(0, B) as b:
                for hf in range(2):
                    g = b * 2 + hf
                    act.wait_ge(s["gu"], g + 1)
                    nc.scalar.activation(sg[:, hf], psg[0:F, hf], ACT.Exp, scale=-1.0).then_inc(s["ex"], 1)
                    act.wait_ge(s["sum"], 2 * g + 2)
                    dst = out[bass.ds(g * CH, CH), :].rearrange("(n p) d -> p n d", p=P)
                    act.dma_start(dst, res[:, hf]).then_inc(s["stored%d" % hf], 16)
            for hf in range(2):
                act.wait_ge(s["stored%d" % hf], 16 * B)

        @block.tensor
        def _(pe):
            pe.wait_ge(s["ld_w"], 48)

            def gates(b, hf, first):
                g = b * 2 + hf
                pe.wait_ge(s["ld%d" % hf], 64 * (b + 1))
                if not first:
                    pe.wait_ge(s["hs"], 4 * (g - 1))
                nc.tensor.matmul(psg[0:F, hf], w_sgu[:, 0:F], x_t[:, hf], start=True, stop=True)
                nc.tensor.matmul(psu[0:F, hf], w_sgu[:, F:2 * F], x_t[:, hf], start=True, stop=True).then_inc(s["gu"], 1)

            def rows(b, hf, first):
                g = b * 2 + hf
                pe.wait_ge(s["hs"], 4 * g + 4)
                if not first:
                    pe.wait_ge(s["sum"], 2 * g - 2)
                for i in range(4):
                    o = psy[:, hf, i * P:(i + 1) * P]
                    nc.tensor.matmul(o, a_t[:, hf, i * P:(i + 1) * P], w_o[:], start=True, stop=False)
                    last = nc.tensor.matmul(o, h_t[:, hf, i * P:(i + 1) * P], w_sdn[:], start=False, stop=True)
                last.then_inc(s["y"], 1)

            gates(0, 0, True)
            gates(0, 1, True)
            rows(0, 0, True)
            gates(1, 0, False)
            rows(0, 1, True)
            with pe.Fori(1, B - 1) as b:
                gates(b, 1, False)
                rows(b, 0, False)
                gates(b + 1, 0, False)
                rows(b, 1, False)
            gates(B - 1, 1, False)
            rows(B - 1, 0, False)
            rows(B - 1, 1, False)

        @block.vector
        def _(dve):
            def chunk(b, hf, first):
                g = b * 2 + hf
                dve.wait_ge(s["ex"], g + 1)
                if not first:
                    dve.wait_ge(s["y"], g - 1)
                    dve.wait_ge(s["stored%d" % hf], 16 * b)
                nc.vector.tensor_scalar(sg1[:, hf], sg[:, hf], 1.0, None, ALU.add).then_inc(s["hs"], 1)
                dve.wait_ge(s["hs"], 4 * g + 1)
                nc.vector.reciprocal(sg[:, hf], sg1[:, hf]).then_inc(s["hs"], 1)
                dve.wait_ge(s["hs"], 4 * g + 2)
                nc.vector.tensor_tensor(sg1[:, hf], psg[0:F, hf], sg[:, hf], ALU.mult).then_inc(s["hs"], 1)
                dve.wait_ge(s["hs"], 4 * g + 3)
                nc.vector.tensor_tensor(h_t[:, hf], psu[0:F, hf], sg1[:, hf], ALU.mult).then_inc(s["hs"], 1)
                dve.wait_ge(s["ld%d" % hf], 64 * (b + 1))
                nc.vector.tensor_tensor(acc[:, hf], x_r[:, hf], r_r[:, hf], ALU.add).then_inc(s["sum"], 1)
                dve.wait_ge(s["sum"], 2 * g + 1)
                dve.wait_ge(s["y"], g + 1)
                nc.vector.tensor_tensor(res[:, hf], psy[:, hf].rearrange("p (n d) -> p n d", n=4), acc[:, hf],
                                        ALU.add).then_inc(s["sum"], 1)

            for hf in range(2):
                chunk(0, hf, True)
            with dve.Fori(1, B) as b:
                for hf in range(2):
                    chunk(b, hf, False)


def kernel(L0_attn_x, L0_attn_Wq, L0_attn_Wk, L0_attn_Wv, L0_attn_Wo, L0_attn_alpha, L0_ffn_router_w, L0_ffn_w_gate,
           L0_ffn_w_up, L0_ffn_w_down, L0_ffn_ws_gate_up, L0_ffn_ws_down):
    import concourse.bacc as bacc
    from concourse.bass_utils import run_bass_kernel_spmd

    def a(v):
        return np.ascontiguousarray(np.asarray(v))

    other = np.arange(D) ^ 1
    consts = np.zeros((P, 449), np.float32)
    row, col = np.arange(P)[:, None], np.arange(P)[None, :]
    consts[:, 0:P] = np.eye(P)
    consts[:, 128:256] = np.where(col > row, np.float32(MASK_D), 0)
    consts[:, 256:384] = np.where(row > col, np.float32(MASK_T), 0)
    consts[:, 384:400] = np.where(row // HD == np.arange(16)[None, :], -0.5, 0)
    consts[:, 416:448] = T - (np.arange(TILES)[None, :] * P + row)
    consts[:, 448] = np.arange(P) % SLOTS
    freq = np.outer(1.0 / 10000.0 ** (np.arange(0, HD, 2)[:HD // 2] / HD), np.arange(S))
    pair = (np.arange(P) % HD) // 2
    sign = np.where(np.arange(P) % 2 == 0, -1.0, 1.0)[:, None]
    rope = np.stack([np.cos(freq)[pair], sign * np.sin(freq)[pair]], 1).astype(np.float32)

    x = a(L0_attn_x).reshape(T, D)
    wq, wk = a(L0_attn_Wq), a(L0_attn_Wk)
    ins = {
        "x": x, "wq": wq, "wqs": a(wq[:, other]), "wk": wk, "wks": a(wk[:, other]), "wv": a(L0_attn_Wv),
        "wo": a(L0_attn_Wo), "alpha": a(np.broadcast_to(a(L0_attn_alpha), (P, 1))), "rwt": a(a(L0_ffn_router_w).T),
        "wgu": a(np.concatenate([a(L0_ffn_w_gate), a(L0_ffn_w_up)], 2)), "wdn": a(L0_ffn_w_down),
        "wsgu": a(L0_ffn_ws_gate_up), "wsdn": a(L0_ffn_ws_down), "consts": consts, "rope": a(rope),
    }
    nc = bacc.Bacc("TRN2", target_bir_lowering=False, num_devices=1)
    aps = {n: nc.dram_tensor("in_" + n, list(v.shape), mybir.dt.from_np(v.dtype), kind="ExternalInput").ap()
           for n, v in ins.items()}
    out = nc.dram_tensor("out", [T, D], F32, kind="ExternalOutput").ap()
    program(nc, out=out, **aps)
    r = run_bass_kernel_spmd(nc, [{"in_" + n: v for n, v in ins.items()}], core_ids=[0])
    return r.results[0]["out"].reshape(B, S, D)
```

```python
from contextlib import ExitStack

import numpy as np
import concourse.bass as bass
from concourse import mybir

F32 = mybir.dt.float32
BF16 = mybir.dt.bfloat16
I32 = mybir.dt.int32
ALU = mybir.AluOpType
ACT = mybir.ActivationFunctionType
AXX = mybir.AxisListType.X

P = 128
B, S, D = 4, 1024, 128
T = B * S
H, HD = 16, 8
E, TOPK, F = 64, 8, 96
SLOTS = 64
ATT_EPS = 1e-5
LN_EPS = 1e-5
TILES = T // P
CH = 512
NCH = T // CH
NPART = 3
GH = 4
QT = S // P
TRIPS = B * H // (2 * GH)
PROD = NPART * NPART * HD
NORM_K = PROD
NORM_Q = 96
DUMMY = SLOTS
ROW = D + E
MASK_D = -1e18
MASK_T = -1e30
ACT_SET = "natural_log_exp_and_others"


def ge(eng, sem, value):
    if isinstance(value, int) and value <= 0:
        return
    eng.wait_ge(sem, value)


def wait_apart(eng, sem, value, passed):
    ge(eng, sem, value)
    eng.sem_inc(passed, 1)


def step_list():
    out = []
    for i in reversed(range(QT)):
        w = P * (i + 1)
        n = 1 if w > 512 else 2 if w > 256 else 4
        pitch = w if n != 2 else 512
        out += [(i, list(range(c, c + n)), pitch) for c in range(0, GH, n)]
    return out


STEPS = step_list()
NS = len(STEPS)
NT = 2 * NS
ROUTE = 19
LEAD = 4


def value_work():
    work = [[] for _ in range(NS)]
    for i in range(QT):
        at = [n for n in range(NS) if STEPS[n][0] == (i - 1 if i else 0)]
        for a, n in enumerate(at):
            work[n].append((i, (i + 1) * a // len(at), (i + 1) * (a + 1) // len(at)))
    return [sorted(w, reverse=True) for w in work]


VALUES = value_work()
HALF_END = [max(n for n in range(NS) if any(w[0] == i for w in VALUES[n])) for i in (QT // 2, 0)]


def program(nc, x, wq, wqs, wk, wks, wv, wo, alpha, rwt, wgu, wdn, wsgu, wsdn, consts, rope, out):
    with ExitStack() as ctx:
        def sb(name, shape, dt=F32, c=ctx):
            return c.enter_context(nc.sbuf_tensor(name, shape, dt))

        def ps(name, shape, c):
            return c.enter_context(nc.psum_tensor(name, shape, F32))

        def sem(name, c=ctx):
            return c.enter_context(nc.semaphore(name))

        qk_parts = nc.dram_tensor("qk_parts", [B, 2, NPART, D, S], BF16, kind="Internal").ap()
        nrm_parts = nc.dram_tensor("nrm_parts", [B, 2, NPART, H, S], BF16, kind="Internal").ap()
        rows = nc.dram_tensor("rows", [T + DUMMY, ROW], F32, kind="Internal").ap()
        routed = nc.dram_tensor("routed", [T + DUMMY, D], F32, kind="Internal").ap()
        sums_d = nc.dram_tensor("sums_d", [TRIPS, 2, GH, S], F32, kind="Internal").ap()
        att_d = nc.dram_tensor("att_d", [TRIPS, 2, GH * HD, S], F32, kind="Internal").ap()

        x_all = sb("x_all", [P, TILES, D])
        xT_all = sb("xT_all", [P, T])
        ident = sb("ident", [P, P])
        identb = sb("identb", [P, P], BF16)
        mask_d = sb("mask_d", [P, P], BF16)
        mask_t = sb("mask_t", [P, P], BF16)
        cst = sb("cst", [P, consts.shape[1]])
        scale = sb("scale", [P, 1])
        v_all = sb("v_all", [P, TRIPS, QT, 64])
        idx64 = sb("idx64", [SLOTS, E], I32)
        idxp = sb("idxp", [P, E // 2], I32)
        q_d = sb("q_d", [P, 2, GH, S], BF16)
        q_s = sb("q_s", [P, 2, GH, S], BF16)
        k_t = sb("k_t", [P, 2, GH, S], BF16)
        ld0, ld1 = sem("ld_qk0"), sem("ld_qk1")
        C_MD, C_MT, C_NB, C_TV, C_SI = 128, 256, 384, 416, 448

        shared = dict(ld0=ld0, ld1=ld1, ident=ident, identb=identb, q_d=q_d, q_s=q_s, k_t=k_t,
                      mask_d=mask_d, mask_t=mask_t, scale=scale, v_all=v_all, idx64=idx64,
                      idxp=idxp, qk_parts=qk_parts, nrm_parts=nrm_parts, rows=rows, routed=routed,
                      xT_all=xT_all, x_all=x_all, att_d=att_d, sums_d=sums_d)
        with ExitStack() as pc:
            w_q = sb("w_q", [P, D], F32, pc)
            w_qs = sb("w_qs", [P, D], F32, pc)
            w_k = sb("w_k", [P, D], F32, pc)
            w_ks = sb("w_ks", [P, D], F32, pc)
            w_v = sb("w_v", [P, D], F32, pc)
            w_r = sb("w_r", [P, E], F32, pc)
            tabs = sb("tabs", [P, 2, S], F32, pc)
            zero = sb("zero", [P, 13 * D], F32, pc)
            st6 = sb("st6", [P, TILES, 6], F32, pc)
            mv = sb("mv", [P, TILES, 2], F32, pc)
            rstd = sb("rstd", [P, TILES], F32, pc)
            al = sb("al", [P, 1], F32, pc)
            xn = sb("xn", [P, 2, 4, D], F32, pc)
            xT = sb("xT", [P, 2, CH], F32, pc)
            ra = sb("ra", [P, 2, CH], F32, pc)
            rb = sb("rb", [P, 2, CH], F32, pc)
            qf = sb("qf", [P, 2, CH], F32, pc)
            res = sb("res", [P, 2, CH], F32, pc)
            sq = sb("sq", [P, 2, CH], F32, pc)
            parts = sb("parts", [P, 2, 2, NPART, CH], BF16, pc)
            nf = sb("nf", [64, CH], F32, pc)
            nres = sb("nres", [64, CH], F32, pc)
            nparts = sb("nparts", [64, 2, NPART, CH], BF16, pc)
            nmax = sb("nmax", [P, 4], F32, pc)
            pe_ = sb("pexp", [P, 4, E], F32, pc)
            top8 = sb("top8", [P, 4, 8], F32, pc)
            mr = sb("mr", [P, 4, E], F32, pc)
            sel = sb("sel", [P, 4, E], F32, pc)
            wsum = sb("wsum", [P, 4], F32, pc)
            rws = sb("rws", [P, 4], F32, pc)
            wts = sb("wts", [P, 2, 4, E], F32, pc)
            selv = sb("selv", [P, 2, 2, E], F32, pc)
            selT = sb("selT", [P, T // 2], F32, pc)
            cand = sb("cand", [P, SLOTS], F32, pc)
            both = sb("both", [E, 2 * SLOTS], F32, pc)
            topv = sb("topv", [E, SLOTS], F32, pc)
            tvc = sb("tvc", [SLOTS, E], F32, pc)
            emp = sb("emp", [SLOTS, E], F32, pc)
            tok = sb("tok", [SLOTS, E], F32, pc)

            with ExitStack() as pp:
                psT = ps("psT", [P, CH], pp)
                psL = ps("psL", [P, CH], pp)
                psV = ps("psV", [P, CH], pp)
                psQ = ps("psQ", [P, 4, CH], pp)
                psN = ps("psN", [P, CH], pp)
                names = ("ld_w ld_c ld_rope consts_cast stat seps lnv rstd_ready zeroed zero_out scl xn_ready "
                         "xT_ps xT_ready lg_ps q_ps k_ps v_ps v_out turned cast resid n_ps n_ready n_cast n_resid "
                         "nmax_ready pexp routing selT_ps selT_ready st_xn0 st_xn1 st_xT0 st_xT1 st_parts0 st_parts1 "
                         "st_nrm0 st_nrm1 st_w0 st_w1 dve_passed sp_passed found tv_ps").split()
                s = {n: sem(n, pp) for n in names}
                XG = 4
                ld_x = [sem("ld_x%d" % i, pp) for i in range(XG)]
                block = pp.enter_context(nc.Block())
                xv = x.rearrange("(n p) d -> p n d", p=P)
                STORES = (("xn", 1), ("xT", 1), ("parts", 1), ("w", 1), ("nrm", 2))

                def chunks(eng, iteration):
                    iteration((0, 0), None)
                    with eng.Fori(0, B - 1) as b:
                        iteration((b, 1), (b, 0))
                        iteration((b + 1, 0), (b, 1))
                    iteration((B - 1, 1), (B - 1, 0))
                    iteration(None, (B - 1, 1))

                @block.sync
                def _(sp):
                    n = TILES // XG
                    sp.dma_start(x_all[:, 0:n, :], xv[:, 0:n, :]).then_inc(ld_x[0], 16)
                    sp.dma_start(cst[:], consts).then_inc(s["ld_c"], 16)
                    for g in range(1, XG):
                        sp.dma_start(x_all[:, g * n:(g + 1) * n, :], xv[:, g * n:(g + 1) * n, :]).then_inc(ld_x[g], 16)
                    sp.wait_ge(s["zeroed"], 1)
                    sp.dma_start(rows[T:T + DUMMY, :], zero[0:DUMMY, 0:ROW]).then_inc(s["zero_out"], 16)
                    step = 13
                    for r in range(0, T + DUMMY, step * P):
                        k = min(step, (T + DUMMY - r) // P)
                        if k:
                            sp.dma_start(routed[r:r + k * P, :].rearrange("(p n) d -> p (n d)", p=P),
                                         zero[:, 0:k * D]).then_inc(s["zero_out"], 16)
                    done = (T + DUMMY) // P * P
                    sp.dma_start(routed[done:T + DUMMY, :], zero[0:T + DUMMY - done, 0:D]).then_inc(s["zero_out"], 16)
                    nz = 2 + -(-(done // P) // step)

                    def stage(b, hf):
                        g = b * 2 + hf
                        sp.wait_ge(s["xn_ready"], g * 4 + 4)
                        sp.dma_start(rows[bass.ds(g * CH, CH), 0:D].rearrange("(n p) d -> p n d", p=P),
                                     xn[:, hf]).then_inc(s["st_xn%d" % hf], 16)
                        wait_apart(sp, s["xT_ready"], g + 2, s["sp_passed"])
                        sp.dma_start(xT_all[:, bass.ds(g * CH, CH)], xT[:, hf]).then_inc(s["st_xT%d" % hf], 16)

                    def after(b, hf):
                        g = b * 2 + hf
                        wait_apart(sp, s["routing"], g * ROUTE + ROUTE, s["sp_passed"])
                        sp.dma_start(rows[bass.ds(g * CH, CH), D:ROW].rearrange("(n p) d -> p n d", p=P),
                                     wts[:, hf]).then_inc(s["st_w%d" % hf], 16)
                        wait_apart(sp, s["resid"], 4 + g * 4 + 4, s["sp_passed"])
                        dst = qk_parts[bass.ds(b, 1), :, :, :, hf * CH:(hf + 1) * CH]
                        sp.dma_start(dst.rearrange("o w a p s -> p (o w a) s"),
                                     parts[:, hf].rearrange("p w a s -> p (w a) s")).then_inc(s["st_parts%d" % hf], 16)
                        wait_apart(sp, s["n_resid"], 2 + g * 2 + 2, s["sp_passed"])
                        for w in range(2):
                            dst = nrm_parts[bass.ds(b, 1), w, :, :, hf * CH:(hf + 1) * CH]
                            sp.dma_start(dst.rearrange("o a h s -> h (o a) s"),
                                         nparts[32 * w:32 * w + H, hf]).then_inc(s["st_nrm%d" % hf], 16)

                    def iteration(cur, prev):
                        if cur:
                            stage(*cur)
                        if prev:
                            after(*prev)

                    chunks(sp, iteration)
                    sp.wait_ge(s["zero_out"], 16 * nz)
                    for hf in range(2):
                        for name, dmas in STORES:
                            sp.wait_ge(s["st_%s%d" % (name, hf)], 16 * dmas * (B + 1))
                    sp.wait_ge(s["zeroed"], 5)
                    for par, ld in enumerate((ld0, ld1)):
                        load_group(sp, shared, ld, 0, 0, par)

                @block.gpsimd
                def _(pool):
                    nc.gpsimd.memset(zero[:], 0.0).then_inc(s["zeroed"], 1)

                    for at, (buf, value) in enumerate(((q_d, 1.0), (q_s, 0.0), (k_t, 0.0))):
                        pool.wait_ge(s["zeroed"], at + 1)
                        nc.gpsimd.memset(buf[64:P], value).then_inc(s["zeroed"], 1)
                    pool.wait_ge(s["zeroed"], 4)
                    nc.gpsimd.memset(k_t[NORM_Q:NORM_Q + NPART], 1.0).then_inc(s["zeroed"], 1)
                    pool.wait_ge(s["zeroed"], 5)

                    def second(b, hf, w):
                        pool.wait_ge(s["cast"], 6 + (b * 2 + hf) * 6 + 3 * w + 1)
                        nc.gpsimd.tensor_tensor(res[:, w], qf[:, w], parts[:, hf, w, 0, :], ALU.subtract).then_inc(s["resid"], 1)

                    def third(b, hf, w):
                        pool.wait_ge(s["cast"], 6 + (b * 2 + hf) * 6 + 3 * w + 3)
                        nc.gpsimd.tensor_tensor(parts[:, hf, w, 2, :], res[:, w], parts[:, hf, w, 1, :],
                                                ALU.subtract).then_inc(s["resid"], 1)

                    def settled(done, n_done):
                        pool.wait_ge(s["resid"], done)
                        ge(pool, s["n_resid"], n_done)

                    def iteration(cur, prev):
                        if prev:
                            third(*prev, 1)
                            gp_ = prev[0] * 2 + prev[1]
                        if cur:
                            second(*cur, 0)
                            g = cur[0] * 2 + cur[1]
                        if prev:
                            settled(4 + gp_ * 4 + 4 + (1 if cur else 0), gp_ * 2 + 2)
                            pool.wait_ge(s["n_cast"], gp_ * 2 + 1)
                            nc.gpsimd.tensor_tensor(nres[:], nf[:], nparts[:, prev[1], 0, :], ALU.subtract).then_inc(s["n_resid"], 1)
                        if cur:
                            if prev:
                                settled(4 + g * 4 + 1, 2 + gp_ * 2 + 1)
                            third(*cur, 0)
                            second(*cur, 1)
                        if prev:
                            settled(4 + gp_ * 4 + 4 + (3 if cur else 0), 2 + gp_ * 2 + 1)
                            pool.wait_ge(s["n_cast"], gp_ * 2 + 2)
                            nc.gpsimd.tensor_tensor(nparts[:, prev[1], 2, :], nres[:], nparts[:, prev[1], 1, :],
                                                    ALU.subtract).then_inc(s["n_resid"], 1)
                            if cur:
                                settled(4 + g * 4 + 3, 2 + gp_ * 2 + 2)

                    chunks(pool, iteration)

                @block.scalar
                def _(act):
                    for dst, src in ((w_r, rwt), (w_q, wq), (w_qs, wqs), (w_k, wk), (w_ks, wks), (w_v, wv), (al, alpha)):
                        act.dma_start(dst[:], src).then_inc(s["ld_w"], 16)
                    act.dma_start(tabs[:], rope).then_inc(s["ld_rope"], 16)
                    act.sem_inc(s["xT_ready"], 1)
                    act.sem_inc(s["pexp"], 4)
                    act.sem_inc(s["v_out"], 1)
                    act.sem_inc(s["cast"], 6)
                    act.sem_inc(s["selT_ready"], 2)
                    for hf in range(2):
                        for name, dmas in STORES:
                            act.sem_inc(s["st_%s%d" % (name, hf)], 16 * dmas)
                    nc.scalar.preload_act_table_set(ACT_SET)
                    act.wait_ge(s["seps"], 1)
                    nc.scalar.activation(rstd[:], rstd[:], ACT.Ln).then_inc(s["lnv"], 1)
                    act.wait_ge(s["lnv"], 1)
                    nc.scalar.activation(rstd[:], rstd[:], ACT.Exp, scale=-0.5).then_inc(s["rstd_ready"], 1)

                    def rows_out(b, hf):
                        g = b * 2 + hf
                        act.wait_ge(s["st_xT%d" % hf], 16 * (b + 1))
                        act.wait_ge(s["xT_ps"], g + 1)
                        nc.scalar.activation(xT[:, hf], psT[:], ACT.Copy).then_inc(s["xT_ready"], 1)

                    def routing(b, hf):
                        act.wait_ge(s["nmax_ready"], b * 2 + hf + 1)
                        for i in range(4):
                            nc.scalar.activation(pe_[:, i, :], psL[:, i * E:(i + 1) * E], ACT.Exp,
                                                 bias=nmax[:, i:i + 1]).then_inc(s["pexp"], 1)

                    def selected(b, hf):
                        g = b * 2 + hf
                        act.wait_ge(s["selT_ps"], g + 1)
                        nc.scalar.activation(selT[:, bass.ds(g * 256, 256)], psT[:, 0:256], ACT.Copy).then_inc(s["selT_ready"], 1)

                    def first(b, hf, w):
                        act.wait_ge(s["st_parts%d" % hf], 16 * (b + 1))
                        act.wait_ge(s["turned"], 6 + (b * 2 + hf) * 6 + 3 * w + 3)
                        nc.scalar.activation(parts[:, hf, w, 0, :], qf[:, w], ACT.Copy).then_inc(s["cast"], 1)
                        nc.scalar.activation(sq[:, w], qf[:, w], ACT.Square).then_inc(s["cast"], 1)

                    def second(b, hf, w):
                        act.wait_ge(s["resid"], 4 + (b * 2 + hf) * 4 + 2 * w + 1)
                        nc.scalar.activation(parts[:, hf, w, 1, :], res[:, w], ACT.Copy).then_inc(s["cast"], 1)

                    def values(b, hf):
                        act.wait_ge(s["v_ps"], b * 2 + hf + 1)
                        dst = v_all[:, bass.ds(b * 2, 2), 4 * hf:4 * hf + 4, :]
                        nc.scalar.activation(dst, psV[:].rearrange("p (i g c) -> p g i c", i=4, g=2),
                                             ACT.Copy).then_inc(s["v_out"], 1)

                    def norm_first(b, hf):
                        act.wait_ge(s["st_nrm%d" % hf], 32 * (b + 1))
                        act.wait_ge(s["n_ready"], b * 2 + hf + 2)
                        nc.scalar.activation(nparts[:, hf, 0, :], nf[:], ACT.Copy).then_inc(s["n_cast"], 1)

                    def norm_second(b, hf):
                        act.wait_ge(s["n_resid"], 2 + (b * 2 + hf) * 2 + 1)
                        nc.scalar.activation(nparts[:, hf, 1, :], nres[:], ACT.Copy).then_inc(s["n_cast"], 1)

                    def iteration(cur, prev):
                        if cur:
                            rows_out(*cur)
                        if prev:
                            second(*prev, 1)
                        if cur:
                            routing(*cur)
                        if prev:
                            selected(*prev)
                        if cur:
                            first(*cur, 0)
                        if prev:
                            norm_first(*prev)
                        if cur:
                            second(*cur, 0)
                            first(*cur, 1)
                        if prev:
                            norm_second(*prev)
                        if cur:
                            values(*cur)

                    chunks(act, iteration)
                    act.wait_ge(s["ld_w"], 16 * 7)
                    nc.scalar.activation(scale[:], al[:], ACT.Exp,
                                         scale=float(np.log(np.sqrt(np.float32(HD)) / np.log(np.float32(1 + HD))))
                                         ).then_inc(s["scl"], 1)

                @block.tensor
                def _(pe):
                    pe.wait_ge(s["ld_c"], 16)
                    pe.wait_ge(s["ld_w"], 16 * 7)

                    def norms(b, hf):
                        g = b * 2 + hf
                        pe.wait_ge(s["cast"], 6 + g * 6 + 5)
                        pe.wait_ge(s["n_ready"], g + 1)
                        for w in range(2):
                            last = nc.tensor.matmul(psN[32 * w:32 * w + 32, :], cst[:, C_NB:C_NB + 32], sq[:, w],
                                                    start=True, stop=True)
                        last.then_inc(s["n_ps"], 1)

                    def turn_selected(b, hf):
                        g = b * 2 + hf
                        pe.wait_ge(s["routing"], g * ROUTE + ROUTE)
                        pe.wait_ge(s["xT_ready"], min(g + 3, NCH + 1) if isinstance(g, int) else g + 3)
                        for j in range(2):
                            last = nc.tensor.transpose(psT[:, j * P:(j + 1) * P],
                                                       selv[:, j].rearrange("p a e -> p (a e)"), cst[:, 0:P])
                        last.then_inc(s["selT_ps"], 1)

                    def stage(b, hf, prev):
                        g = b * 2 + hf
                        pe.wait_ge(s["xn_ready"], g * 4 + 4)
                        pe.wait_ge(s["xT_ready"], g + 1)
                        pe.wait_ge(s["selT_ready"], g + 1)
                        for i in range(4):
                            last = nc.tensor.transpose(psT[:, i * P:(i + 1) * P], xn[:, hf, i, :], cst[:, 0:P])
                        last.then_inc(s["xT_ps"], 1)
                        if prev:
                            norms(*prev)
                        pe.wait_ge(s["xT_ready"], g + 2)
                        pe.wait_ge(s["pexp"], g * 4 + 4)
                        for i in range(4):
                            last = nc.tensor.matmul(psL[:, i * E:(i + 1) * E], xT[:, hf, i * P:(i + 1) * P], w_r[:],
                                                    start=True, stop=True)
                        last.then_inc(s["lg_ps"], 1)
                        if prev:
                            turn_selected(*prev)
                        for w, (wa, wb) in enumerate(((w_q, w_qs), (w_k, w_ks))):
                            pe.wait_ge(s["turned"], g * 6 + 3 * w + 2)
                            nc.tensor.matmul(psQ[:, 2 * w, :], wa[:], xT[:, hf], start=True, stop=True)
                            nc.tensor.matmul(psQ[:, 2 * w + 1, :], wb[:], xT[:, hf], start=True, stop=True)\
                                .then_inc(s["k_ps" if w else "q_ps"], 1)
                        pe.wait_ge(s["v_out"], g + 1)
                        for i in range(4):
                            last = nc.tensor.matmul(psV[:, i * P:(i + 1) * P], xT[:, hf, i * P:(i + 1) * P], w_v[:],
                                                    start=True, stop=True)
                        last.then_inc(s["v_ps"], 1)

                    def iteration(cur, prev):
                        if cur:
                            stage(*cur, prev)
                        else:
                            norms(*prev)
                            turn_selected(*prev)

                    chunks(pe, iteration)
                    pe.wait_ge(s["found"], 2 * (SLOTS // 8) * 2 + 2)
                    nc.tensor.transpose(psT[0:SLOTS, 0:E], topv[:], cst[0:E, 0:E]).then_inc(s["tv_ps"], 1)

                @block.vector
                def _(dve):
                    dve.sem_inc(s["turned"], 6)
                    dve.sem_inc(s["resid"], 4)
                    dve.sem_inc(s["n_ready"], 1)
                    dve.sem_inc(s["n_resid"], 2)
                    dve.wait_ge(s["ld_c"], 16)
                    for dst, c0 in ((identb, 0), (mask_d, C_MD), (mask_t, C_MT), (ident, 0)):
                        nc.vector.tensor_copy(dst[:], cst[:, c0:c0 + P]).then_inc(s["consts_cast"], 1)
                    for n in range(TILES):
                        if n % (TILES // XG) == 0:
                            dve.wait_ge(ld_x[n // (TILES // XG)], 16)
                        nc.vector.bn_stats(st6[:, n, :], x_all[:, n, :]).then_inc(s["stat"], 1)
                    for n in range(TILES):
                        if n == 0:
                            dve.wait_ge(s["stat"], TILES)
                        nc.vector.bn_aggr(mv[:, n, :], st6[:, n, :]).then_inc(s["stat"], 1)
                    dve.wait_ge(s["stat"], 2 * TILES)
                    nc.vector.tensor_scalar(rstd[:], mv[:, :, 1], LN_EPS, None, ALU.add).then_inc(s["seps"], 1)
                    dve.wait_ge(s["rstd_ready"], 1)

                    def normalise(b, hf):
                        g = b * 2 + hf
                        dve.wait_ge(s["st_xn%d" % hf], 16 * (b + 1))
                        if not isinstance(g, int):
                            dve.wait_ge(s["xT_ps"], g - 1)
                        elif g >= 2:
                            dve.wait_ge(s["xT_ps"], g - 1)
                        for i in range(4):
                            n = g * 4 + i
                            nc.vector.tensor_scalar(xn[:, hf, i, :], x_all[:, bass.ds(n, 1), :].rearrange("p o d -> p (o d)"),
                                                    mv[:, bass.ds(n, 1), 0], rstd[:, bass.ds(n, 1)],
                                                    ALU.subtract, ALU.mult).then_inc(s["xn_ready"], 1)

                    def stage(b, hf, following):
                        g = b * 2 + hf
                        dve.wait_ge(s["lg_ps"], g + 1)
                        dve.wait_ge(s["pexp"], g * 4 + 4)
                        nc.vector.tensor_reduce(nmax[:], psL[:, 0:256].rearrange("p (i e) -> p i e", i=4), AXX, ALU.max,
                                                negate=True).then_inc(s["nmax_ready"], 1)
                        if following:
                            normalise(*following)
                        for w in range(2):
                            dve.wait_ge(s["k_ps" if w else "q_ps"], g + 1)
                            nc.vector.tensor_tensor(ra[:, w], psQ[:, 2 * w, :], tabs[:, 0, hf * CH:(hf + 1) * CH],
                                                    ALU.mult).then_inc(s["turned"], 1)
                            nc.vector.tensor_tensor(rb[:, w], psQ[:, 2 * w + 1, :], tabs[:, 1, hf * CH:(hf + 1) * CH],
                                                    ALU.mult).then_inc(s["turned"], 1)
                            dve.wait_ge(s["turned"], 6 + g * 6 + 3 * w + 2)
                            dve.wait_ge(s["cast"], g * 6 + 3 * w + 2)
                            dve.wait_ge(s["resid"], g * 4 + 2 * w + 1)
                            nc.vector.tensor_tensor(qf[:, w], ra[:, w], rb[:, w], ALU.add).then_inc(s["turned"], 1)

                    def after(b, hf):
                        g = b * 2 + hf
                        count = [0]

                        def mark(ins):
                            ins.then_inc(s["routing"], 1)
                            count[0] += 1

                        def settled():
                            wait_apart(dve, s["routing"], g * ROUTE + count[0], s["dve_passed"])
                        wait_apart(dve, s["pexp"], g * 4 + 8, s["dve_passed"])
                        for i in range(4):
                            mark(nc.vector.max(top8[:, i, :], pe_[:, i, :]))
                        settled()
                        for i in range(4):
                            mark(nc.vector.match_replace(mr[:, i, :], top8[:, i, :], pe_[:, i, :], -1.0))
                        mark(nc.vector.reduce_sum(wsum[:], top8[:], AXX))
                        settled()
                        mark(nc.vector.tensor_scalar(sel[:], mr[:], 0.0, None, ALU.is_lt))
                        mark(nc.vector.reciprocal(rws[:], wsum[:]))
                        dve.wait_ge(s["selT_ready"], g + 2)
                        settled()
                        for i in range(4):
                            mark(nc.vector.tensor_scalar(selv[:, i % 2, i // 2, :], sel[:, i, :],
                                                         cst[:, bass.ds(C_TV + g * 4 + i, 1)], None, ALU.mult))
                        dve.wait_ge(s["st_w%d" % hf], 16 * (b + 1))
                        for i in range(4):
                            mark(nc.vector.scalar_tensor_tensor(wts[:, hf, i, :], pe_[:, i, :], rws[:, i:i + 1], sel[:, i, :],
                                                                ALU.mult, ALU.mult))
                        assert count[0] == ROUTE

                    def norm(b, hf):
                        g = b * 2 + hf
                        dve.wait_ge(s["n_ps"], g + 1)
                        dve.wait_ge(s["n_resid"], g * 2 + 1)
                        nc.vector.tensor_scalar(nf[:], psN[0:64, :], -0.25 * ATT_EPS, None, ALU.add).then_inc(s["n_ready"], 1)

                    normalise(0, 0)
                    dve.wait_ge(s["ld_rope"], 16)
                    def iteration(cur, prev):
                        if cur:
                            b, hf = cur
                            if isinstance(b, int) and b * 2 + hf == NCH - 1:
                                stage(b, hf, None)
                            else:
                                stage(b, hf, (b + hf, 1 - hf))
                        if prev:
                            norm(*prev)
                        if cur:
                            after(*cur)

                    chunks(dve, iteration)

                    n = 0

                    def done(ins):
                        nonlocal n
                        n += 1
                        ins.then_inc(s["found"], 1)
                        dve.wait_ge(s["found"], n)

                    dve.wait_ge(s["selT_ready"], NCH + 2)
                    for r in range(SLOTS // 8):
                        m = cand[:, 8 * r:8 * r + 8]
                        done(nc.vector.max(m, selT[:]))
                        done(nc.vector.match_replace(selT[:], m, selT[:], 0.0))
                    done(nc.vector.tensor_copy(both[:, 0:SLOTS], cand[0:E, :]))
                    done(nc.vector.tensor_copy(both[:, SLOTS:2 * SLOTS], cand[E:P, :]))
                    for r in range(SLOTS // 8):
                        m = topv[:, 8 * r:8 * r + 8]
                        done(nc.vector.max(m, both[:]))
                        done(nc.vector.match_replace(both[:], m, both[:], 0.0))
                    dve.wait_ge(s["tv_ps"], 1)
                    done(nc.vector.tensor_scalar(emp[:], psT[0:SLOTS, 0:E], 0.0, cst[0:SLOTS, C_SI:C_SI + 1],
                                                 ALU.is_equal, ALU.mult))
                    done(nc.vector.tensor_scalar(tok[:], psT[0:SLOTS, 0:E], -1.0, float(T), ALU.mult, ALU.add))
                    done(nc.vector.tensor_tensor(tok[:], tok[:], emp[:], ALU.add))
                    done(nc.vector.tensor_copy(idx64[:], tok[:]))
                    pairs = tok[:].rearrange("c (r o) -> c o r", o=2)
                    done(nc.vector.tensor_copy(idxp[0:SLOTS, :], pairs[:, 0, :]))
                    done(nc.vector.tensor_copy(idxp[SLOTS:P, :], pairs[:, 1, :]))

        attend(nc, shared, wgu, wdn)
        output(nc, shared, wo, wsgu, wsdn, out)



def load_group(sp, m, ld, b, gp, par):
    q_d, q_s, k_t = m["q_d"], m["q_s"], m["k_t"]
    h0 = 8 * gp + GH * par
    src = m["qk_parts"][bass.ds(b, 1)].rearrange("o w a (h d) s -> (o w) a d h s", d=HD)
    nrm = m["nrm_parts"][bass.ds(b, 1)].rearrange("o w a h s -> (o w) a h s")
    for a in range(NPART):
        k0 = a * NPART * HD
        for c in range(NPART):
            r = k0 + c * HD
            qa = src[0, a, :, h0:h0 + GH, :]
            sp.dma_start(q_d[r:r + HD, par], qa).then_inc(ld, 16)
            sp.dma_start(q_s[r:r + HD, par], qa).then_inc(ld, 16)
            sp.dma_start(k_t[r:r + HD, par], src[1, c, :, h0:h0 + GH, :]).then_inc(ld, 16)
    sp.dma_start(q_d[NORM_Q:NORM_Q + NPART, par], nrm[0, :, h0:h0 + GH, :]).then_inc(ld, 16)
    sp.dma_start(k_t[NORM_K:NORM_K + NPART, par], nrm[1, :, h0:h0 + GH, :]).then_inc(ld, 16)


def attend(nc, m, wgu, wdn):
    with ExitStack() as ctx:
        def sb(name, shape, dt=F32):
            return ctx.enter_context(nc.sbuf_tensor(name, shape, dt))

        def ps(name, shape):
            return ctx.enter_context(nc.psum_tensor(name, shape, F32))

        q_d, q_s, k_t = m["q_d"], m["q_s"], m["k_t"]
        v_aug = sb("v_aug", [P, 2, QT, GH, 32])
        r_buf = sb("r_buf", [P, 2, S])
        z_buf = sb("z_buf", [P, 4, S])
        m_buf = sb("m_buf", [P, 8, GH])
        p_buf = sb("p_buf", [P, 2, GH, S])
        one = sb("one", [P, 1])
        o_n = sb("o_n", [P, 2, CH])
        xg = sb("xg", [P, 2, ROW])
        xgT = sb("xgT", [P, P])
        w_gu = sb("w_gu", [P, 2, 2, 2 * F])
        w_dn = sb("w_dn", [F, 2, 2, D])
        h_a = sb("h_a", [P, F])
        h_b = sb("h_b", [P, F])
        hT = sb("hT", [F, P])
        ys = sb("ys", [2 * SLOTS, 2, D])
        gidx = sb("gidx", [P, 2, 1], I32)
        sidx = sb("sidx", [SLOTS, 2, 2], I32)

        ps_d = ps("ps_d", [P, S])
        ps_s = ps("ps_s", [P, S])
        ps_t = ps("ps_t", [P, S])
        ps_o = ps("ps_o", [P, CH])
        ps_m = ps("ps_m", [P, CH])

        names = ("d_ready s_ready ln_done r_ready z_done m_done u_ready t_ready p_done pv_done "
                 "o_out ones o_stored0 o_stored1 v_loaded v_clear ld_w0 ld_w1 x_idx x_got0 x_got1 xT_ps xT_ok gu_ps "
                 "gu_exp h_step hT_ps hT_ok y_ps y_ok sc_idx scat dve_passed sp_passed pool_passed").split()
        s = {n: ctx.enter_context(nc.semaphore("b_" + n)) for n in names}
        s.update(ld0=m["ld0"], ld1=m["ld1"])
        block = ctx.enter_context(nc.Block())
        LOADS = 3 * NPART * NPART + 2
        PAIR_AT = NT // 4
        PV0, YPS0, YOK0, PD0 = 9, 2, 2, 1

        def seg(buf, step):
            i, heads, pitch = step
            return buf[:, 0:len(heads) * pitch].rearrange("p (c w) -> p c w", c=len(heads))[:, :, 0:P * (i + 1)]

        def unit_of(n):
            return 8 * (n // NS) + (QT - 1 - STEPS[n % NS][0])

        def trips(eng, lead, stages):
            def iteration(t, n, last):
                for ahead, stage in stages:
                    if n + ahead < NT:
                        stage(t, n + ahead)
                    elif not last:
                        stage(t + 1, n + ahead - NT)

            for n in range(-lead, 0):
                for ahead, stage in stages:
                    if n + ahead >= 0:
                        stage(0, n + ahead)
            with eng.Fori(0, TRIPS - 1) as t:
                for n in range(NT):
                    iteration(t, n, False)
            for n in range(NT):
                iteration(TRIPS - 1, n, True)

        @block.sync
        def _(sp):
            def weights(t, p):
                ld = s["ld_w%d" % (p % 2)]
                wait_apart(sp, s["y_ps"], YPS0 + t * 4 + p - 1, s["sp_passed"])
                e0 = t * 8 + 2 * p
                sp.dma_start(w_gu[:, p % 2], wgu[bass.ds(e0, 2)].rearrange("e d f -> d e f")).then_inc(ld, 16)
                sp.dma_start(w_dn[:, p % 2], wdn[bass.ds(e0, 2)].rearrange("e f d -> f e d")).then_inc(ld, 16)

            def store(t, k):
                par, hh = k // 2, k % 2
                wait_apart(sp, s["o_out"], t * 4 + k + 2, s["sp_passed"])
                cols = slice(CH * (1 - hh), CH * (2 - hh))
                for c in range(GH):
                    dst = m["att_d"][bass.ds(t, 1), par, c * HD:(c + 1) * HD, cols].rearrange("o r q -> (o r) q")
                    sp.dma_start(dst, o_n[32 * c:32 * c + HD, hh, :]).then_inc(s["o_stored%d" % hh], 16)
                dst = m["sums_d"][bass.ds(t, 1), par, :, cols].rearrange("o c q -> (o c) q")
                sp.dma_start(dst, o_n[HD:P:32, hh, :]).then_inc(s["o_stored%d" % hh], 16)

            def trip(b, gp, last):
                t = b * 2 + gp
                after = (b, 1) if gp == 0 else (b + 1, 0)
                weights(t, 2)
                store(t, 0)
                if not last:
                    wait_apart(sp, s["s_ready"], t * NT + NS, s["sp_passed"])
                    load_group(sp, m, s["ld0"], *after, 0)
                weights(t, 3)
                store(t, 1)
                if not last:
                    weights(t + 1, 0)
                store(t, 2)
                if not last:
                    wait_apart(sp, s["s_ready"], t * NT + NT, s["sp_passed"])
                    load_group(sp, m, s["ld1"], *after, 1)
                    weights(t + 1, 1)
                store(t, 3)

            weights(0, 0)
            weights(0, 1)
            with sp.Fori(0, B - 1) as b:
                trip(b, 0, False)
                trip(b, 1, False)
            trip(B - 1, 0, False)
            trip(B - 1, 1, True)
            for hh in range(2):
                sp.wait_ge(s["o_stored%d" % hh], 16 * (GH + 1) * (1 + 2 * TRIPS))

        @block.gpsimd
        def _(pool):
            for par in range(2):
                nc.gpsimd.memset(v_aug[:, par], 0.0).then_inc(s["v_clear"], 1)
            pool.wait_ge(s["v_clear"], 2)
            for par in range(2):
                nc.gpsimd.memset(v_aug[:, par, :, :, HD], 1.0).then_inc(s["v_clear"], 1)

            def values(t, par):
                pool.wait_ge(s["pv_done"], PV0 + t * 16 + 8 * par - 8)
                src = m["v_all"][:, bass.ds(t, 1), :, 32 * par:32 * par + 32].rearrange("p o j (c d) -> p (o j) c d", c=GH)
                nc.gpsimd.tensor_copy(v_aug[:, par, :, :, 0:HD], src).then_inc(s["v_loaded"], 1)

            def gather(t, p):
                g = t * 4 + p
                pool.wait_ge(s["y_ok"], YOK0 + g - 1)
                nc.gpsimd.tensor_copy(gidx[:, p % 2], m["idxp"][:, bass.ds(g, 1)]).then_inc(s["x_idx"], 1)
                wait_apart(pool, s["x_idx"], g + 1, s["pool_passed"])
                nc.gpsimd.indirect_dma_start(xg[:, p % 2], None, m["rows"], bass.IndirectOffsetOnAxis(gidx[:, p % 2], 0)
                                             ).then_inc(s["x_got%d" % (p % 2)], 16)

            def added(t, p, e):
                wait_apart(pool, s["scat"], 16 * (2 * (t * 4 + p) + e + 1), s["pool_passed"])

            def scatter(t, p, e):
                g = t * 4 + p
                if e == 0:
                    nc.gpsimd.tensor_copy(sidx[:, p % 2], m["idx64"][:, bass.ds(2 * g, 2)]).then_inc(s["sc_idx"], 1)
                    wait_apart(pool, s["sc_idx"], g + 1, s["pool_passed"])
                    wait_apart(pool, s["y_ok"], YOK0 + g + 1, s["pool_passed"])
                else:
                    added(t, p, 0)
                nc.gpsimd.indirect_dma_start(m["routed"], bass.IndirectOffsetOnAxis(sidx[:, p % 2, e:e + 1], 0),
                                             ys[SLOTS * e:SLOTS * (e + 1), p % 2, :], None, compute_op=ALU.add).then_inc(s["scat"], 16)

            def shift(t, n):
                g = t * NT + n
                if n % NS == 0:
                    values(t, n // NS)
                pool.wait_ge(s["m_done"], g + 1)
                step = STEPS[n % NS]
                k = len(step[1])
                z = seg(z_buf[:, n % 4], step)
                nc.gpsimd.tensor_tensor(z, z, m_buf[:, n % 8, 0:k].unsqueeze(2).to_broadcast([P, k, P * (step[0] + 1)]),
                                        ALU.subtract).then_inc(s["u_ready"], 1)

            def experts(t, n):
                q, r = n % PAIR_AT, n // PAIR_AT
                if q == 0:
                    gather(t, r)
                if q == 7:
                    scatter(t, r, 0)
                if q == 8:
                    scatter(t, r, 1)
                if q == 9:
                    added(t, r, 1)

            trips(pool, 2, ((2, shift), (0, experts)))

        @block.scalar
        def _(act):
            nc.scalar.preload_act_table_set(ACT_SET)

            act.sem_inc(s["p_done"], PD0)

            def log(t, n):
                g = t * NT + n
                step = STEPS[n % NS]
                ge(act, s["z_done"], g - 1)
                act.wait_ge(s["d_ready"], g + 1)
                nc.scalar.activation(seg(r_buf[:, n % 2], step), seg(ps_d, step), ACT.Ln, scale=-2.0).then_inc(s["ln_done"], 1)

            def root(t, n):
                g = t * NT + n
                step = STEPS[n % NS]
                r = seg(r_buf[:, n % 2], step)
                act.wait_ge(s["ln_done"], g + 1)
                nc.scalar.activation(r, r, ACT.Exp, scale=-0.5).then_inc(s["r_ready"], 1)

            def probs(t, n):
                g = t * NT + n
                step = STEPS[n % NS]
                i, heads, _ = step
                u = unit_of(n)
                act.wait_ge(s["t_ready"], g + 1)
                act.wait_ge(s["pv_done"], PV0 + t * 16 + u - 1)
                nc.scalar.activation(p_buf[:, u % 2, heads[0]:heads[-1] + 1, 0:P * (i + 1)], seg(ps_t, step),
                                     ACT.Exp).then_inc(s["p_done"], 1)

            def experts(t, n, at):
                g = t * 4 + n // PAIR_AT
                if at == 0:
                    act.wait_ge(s["gu_ps"], g + 1)
                    nc.scalar.activation(h_a[:], ps_m[:, 128:128 + F], ACT.Exp, scale=-1.0).then_inc(s["gu_exp"], 1)
                if at == 1:
                    act.wait_ge(s["gu_exp"], g * 3 + 1)
                    nc.scalar.activation(h_a[:], h_a[:], ACT.Ln, bias=one[:]).then_inc(s["gu_exp"], 1)
                if at == 2:
                    act.wait_ge(s["gu_exp"], g * 3 + 2)
                    nc.scalar.activation(h_a[:], h_a[:], ACT.Exp, scale=-1.0).then_inc(s["gu_exp"], 1)

            def sigmoid(q, at):
                return lambda t, n: experts(t, n, at) if n % PAIR_AT == q else None

            act.wait_ge(s["ones"], 1)
            trips(act, LEAD, ((LEAD, log), (0, sigmoid(4, 1)), (0, probs), (0, sigmoid(4, 2)), (LEAD, root),
                              (0, sigmoid(3, 0))))

        @block.tensor
        def _(pe):
            pe.sem_inc(s["pv_done"], PV0)
            pe.sem_inc(s["y_ps"], YPS0)

            def products(out, qs, t, n):
                g = t * NT + n
                par, (i, heads, pitch) = n // NS, STEPS[n % NS]
                w = P * (i + 1)
                for a, c in enumerate(heads):
                    for k0 in range(0, w, CH):
                        k1 = min(w, k0 + CH)
                        diag = out is ps_d and k1 == w
                        last = nc.tensor.matmul(out[:, a * pitch + k0:a * pitch + k1], qs[:, par, c, i * P:(i + 1) * P],
                                                k_t[:, par, c, k0:k1], start=True, stop=not diag)
                        if diag:
                            last = nc.tensor.matmul(out[:, a * pitch + w - P:a * pitch + w], m["identb"][:], m["mask_d"][:],
                                                    start=False, stop=True)
                return last

            def distances(t, n):
                if n % NS == 0:
                    pe.wait_ge(s["ld%d" % (n // NS)], (t + 1) * 16 * LOADS)
                ge(pe, s["ln_done"], t * NT + n)
                products(ps_d, q_d, t, n).then_inc(s["d_ready"], 1)

            def scores(t, n):
                ge(pe, s["z_done"], t * NT + n)
                products(ps_s, q_s, t, n).then_inc(s["s_ready"], 1)

            def values(t, n):
                par = n // NS
                for i, j0, j1 in VALUES[n % NS]:
                    u = 8 * par + QT - 1 - i
                    if j0 == 0:
                        end = par * NS + max(a for a in range(NS) if STEPS[a][0] == i)
                        pe.wait_ge(s["p_done"], PD0 + t * NT + end + 1)
                        if i == QT - 1:
                            pe.wait_ge(s["v_loaded"], t * 2 + par + 1)
                        if i % 4 == 3:
                            pe.wait_ge(s["o_out"], t * 4 + u // 4 + 1)
                    for j in range(j0, j1):
                        for c in range(GH):
                            last = nc.tensor.matmul(ps_o[32 * c:32 * c + 32, (i % 4) * P:(i % 4 + 1) * P],
                                                    v_aug[:, par, j, c, :], p_buf[:, u % 2, c, j * P:(j + 1) * P],
                                                    start=j == 0, stop=j == i)
                    if j1 == i + 1:
                        last.then_inc(s["pv_done"], 1)

            def turn(t, n):
                g = t * NT + n
                i, heads, pitch = STEPS[n % NS]
                pe.wait_ge(s["u_ready"], g + 1)
                pe.wait_ge(s["p_done"], PD0 + g)
                for a in range(len(heads)):
                    for j in range(i + 1):
                        o = a * pitch + j * P
                        diag = j == i
                        last = nc.tensor.matmul(ps_t[:, o:o + P], z_buf[:, n % 4, o:o + P], m["ident"][:], start=True,
                                                stop=not diag, is_transpose=True)
                        if diag:
                            last = nc.tensor.matmul(ps_t[:, o:o + P], m["identb"][:], m["mask_t"][:], start=False, stop=True)
                last.then_inc(s["t_ready"], 1)

            def experts(t, n):
                q, p = n % PAIR_AT, n // PAIR_AT
                g = t * 4 + p
                if q == 2:
                    pe.wait_ge(s["x_got%d" % (p % 2)], 16 * (t * 2 + p // 2 + 1))
                    pe.wait_ge(s["y_ok"], YOK0 + g)
                    nc.tensor.transpose(ps_m[:, 0:P], xg[:, p % 2, 0:D], m["ident"][:]).then_inc(s["xT_ps"], 1)
                if q == 3:
                    pe.wait_ge(s["ld_w%d" % (p % 2)], 32 * (t * 2 + p // 2 + 1))
                    pe.wait_ge(s["xT_ok"], g + 1)
                    for e in range(2):
                        last = nc.tensor.matmul(ps_m[SLOTS * e:SLOTS * (e + 1), 128:128 + 2 * F],
                                                xgT[:, SLOTS * e:SLOTS * (e + 1)], w_gu[:, p % 2, e, :], start=True, stop=True)
                    last.then_inc(s["gu_ps"], 1)
                if q == 5:
                    pe.wait_ge(s["h_step"], g * 3 + 3)
                    nc.tensor.transpose(ps_m[0:F, 320:448], h_a[:], m["ident"][:]).then_inc(s["hT_ps"], 1)
                if q == 6:
                    pe.wait_ge(s["hT_ok"], g + 1)
                    for e in range(2):
                        last = nc.tensor.matmul(ps_m[SLOTS * e:SLOTS * (e + 1), 0:D], hT[:, SLOTS * e:SLOTS * (e + 1)],
                                                w_dn[:, p % 2, e, :], start=True, stop=True)
                    last.then_inc(s["y_ps"], 1)

            trips(pe, LEAD, ((LEAD, distances), (LEAD - 1, scores), (0, turn), (0, experts), (0, values)))

        @block.vector
        def _(dve):
            dve.sem_inc(s["o_out"], 1)
            nc.vector.memset(one[:], 1.0).then_inc(s["ones"], 1)
            dve.sem_inc(s["y_ok"], YOK0)
            for hh in range(2):
                dve.sem_inc(s["o_stored%d" % hh], 16 * (GH + 1))

            def ratios(t, n):
                g = t * NT + n
                step = STEPS[n % NS]
                dve.wait_ge(s["r_ready"], g + 1)
                dve.wait_ge(s["s_ready"], g + 1)
                nc.vector.tensor_tensor(seg(z_buf[:, n % 4], step), seg(ps_s, step), seg(r_buf[:, n % 2], step),
                                        ALU.mult).then_inc(s["z_done"], 1)

            def squares(t, n):
                g = t * NT + n
                step = STEPS[n % NS]
                wait_apart(dve, s["z_done"], g + 1, s["dve_passed"])
                z = seg(z_buf[:, n % 4], step)
                for a in range(len(step[1])):
                    last = nc.vector.tensor_tensor_reduce(out=z[:, a], in0=z[:, a], in1=z[:, a], scale=m["scale"][:], scalar=0.0,
                                                          op0=ALU.mult, op1=ALU.max, accum_out=m_buf[:, n % 8, a:a + 1])
                last.then_inc(s["m_done"], 1)

            def sums_out(t, n):
                par, hh = n // NS, HALF_END.index(n % NS)
                dve.wait_ge(s["pv_done"], PV0 + t * 16 + 8 * par + 4 * hh + 4)
                dve.wait_ge(s["o_stored%d" % hh], 16 * (GH + 1) * (2 * t + par + 1))
                nc.vector.tensor_copy(o_n[:, hh], ps_o[:]).then_inc(s["o_out"], 1)

            def experts(t, n):
                q, p = n % PAIR_AT, n // PAIR_AT
                g = t * 4 + p
                if q == 2:
                    dve.wait_ge(s["xT_ps"], g + 1)
                    nc.vector.tensor_copy(xgT[:], ps_m[:, 0:P]).then_inc(s["xT_ok"], 1)
                if q == 4:
                    dve.wait_ge(s["gu_exp"], g * 3 + 3)
                    nc.vector.tensor_tensor(h_b[:], ps_m[:, 128:128 + F], h_a[:], ALU.mult).then_inc(s["h_step"], 1)
                    dve.wait_ge(s["h_step"], g * 3 + 1)
                    for e in range(2):
                        a, b = SLOTS * e, SLOTS * (e + 1)
                        nc.vector.scalar_tensor_tensor(h_a[a:b], ps_m[a:b, 128 + F:128 + 2 * F],
                                                       xg[a:b, p % 2, bass.ds(D + 2 * g + e, 1)], h_b[a:b],
                                                       ALU.mult, ALU.mult).then_inc(s["h_step"], 1)
                if q == 5:
                    dve.wait_ge(s["hT_ps"], g + 1)
                    nc.vector.tensor_copy(hT[:], ps_m[0:F, 320:448]).then_inc(s["hT_ok"], 1)
                if q == 6:
                    dve.wait_ge(s["y_ps"], YPS0 + g + 1)
                    nc.vector.tensor_copy(ys[:, p % 2], ps_m[:, 0:D]).then_inc(s["y_ok"], 1)

            def rest(t, n):
                if n % NS in HALF_END:
                    sums_out(t, n)
                experts(t, n)

            trips(dve, LEAD - 1, ((LEAD - 1, ratios), (LEAD - 1, squares), (0, rest)))


def output(nc, m, wo, wsgu, wsdn, out):
    with ExitStack() as ctx:
        def sb(name, shape, dt=F32):
            return ctx.enter_context(nc.sbuf_tensor(name, shape, dt))

        def ps(name, shape):
            return ctx.enter_context(nc.psum_tensor(name, shape, F32))

        w_o = sb("w_o", [P, D])
        w_sgu = sb("w_sgu", [P, 2 * F])
        w_sdn = sb("w_sdn", [F, D])
        a_t = sb("a_t", [P, 2, CH])
        s_t = sb("s_t", [P, 2, CH])
        a_n = sb("a_n", [P, 2, CH])
        r_r = sb("r_r", [P, 2, 4, D])
        sg = sb("sg", [F, 2, CH])
        sg1 = sb("sg1", [F, 2, CH])
        h_t = sb("h_t", [F, 2, CH])
        acc = sb("acc", [P, 2, 4, D])
        res = sb("res_out", [P, 2, 4, D])
        psg = ps("psg", [P, 2, CH])
        psu = ps("psu", [P, 2, CH])
        psy = ps("psy", [P, 2, CH])
        one = sb("one_out", [P, 1])
        s = {n: ctx.enter_context(nc.semaphore("c_" + n)) for n in
             "ld_w ld_a0 ld_a1 ld_r0 ld_r1 inv norm gu ex hs y add sum one stored0 stored1 passed".split()}
        block = ctx.enter_context(nc.Block())

        def chunks(eng, chunk):
            with eng.Fori(0, B) as b:
                for hf in range(2):
                    chunk(b, hf)

        @block.sync
        def _(sp):
            for dst, src in ((w_o, wo), (w_sgu, wsgu), (w_sdn, wsdn)):
                sp.dma_start(dst[:], src).then_inc(s["ld_w"], 16)

            def load_att(b, hf):
                src = m["att_d"][bass.ds(2 * b, 2), :, :, hf * CH:(hf + 1) * CH].rearrange("g p r q -> (g p r) q")
                sp.dma_start(a_t[:, hf], src).then_inc(s["ld_a%d" % hf], 16)
                src = m["sums_d"][bass.ds(2 * b, 2), :, :, hf * CH:(hf + 1) * CH].rearrange("g p c q -> (g p c) q")
                sp.dma_start(s_t[:, hf], src.unsqueeze(1).to_broadcast([H, HD, CH])).then_inc(s["ld_a%d" % hf], 16)

            def load_routed(b, hf):
                src = m["routed"][bass.ds((2 * b + hf) * CH, CH), :]
                sp.dma_start(r_r[:, hf], src.rearrange("(n p) d -> p n d", p=P)).then_inc(s["ld_r%d" % hf], 16)

            def store(b, hf):
                g = b * 2 + hf
                wait_apart(sp, s["sum"], g + 3, s["passed"])
                dst = out[bass.ds(g * CH, CH), :].rearrange("(n p) d -> p n d", p=P)
                sp.dma_start(dst, res[:, hf]).then_inc(s["stored%d" % hf], 16)

            for hf in range(2):
                load_att(0, hf)
                load_routed(0, hf)
            with sp.Fori(0, B - 1) as b:
                for hf in range(2):
                    g = b * 2 + hf
                    wait_apart(sp, s["add"], g + 1, s["passed"])
                    load_routed(b + 1, hf)
                    wait_apart(sp, s["norm"], g + 1, s["passed"])
                    load_att(b + 1, hf)
                    store(b, hf)
            for hf in range(2):
                store(B - 1, hf)
            for hf in range(2):
                sp.wait_ge(s["stored%d" % hf], 16 * (B + 1))

        @block.scalar
        def _(act):
            nc.scalar.preload_act_table_set(ACT_SET)
            act.wait_ge(s["one"], 1)

            def sigmoid(b, hf):
                g = b * 2 + hf
                act.wait_ge(s["hs"], 2 * g + 2)
                act.wait_ge(s["gu"], g + 1)
                nc.scalar.activation(sg[:, hf], psg[0:F, hf], ACT.Exp, scale=-1.0).then_inc(s["ex"], 1)
                act.wait_ge(s["ex"], 3 * g + 1)
                nc.scalar.activation(sg[:, hf], sg[:, hf], ACT.Ln, bias=one[0:F]).then_inc(s["ex"], 1)
                act.wait_ge(s["ex"], 3 * g + 2)
                nc.scalar.activation(sg1[:, hf], sg[:, hf], ACT.Exp, scale=-1.0).then_inc(s["ex"], 1)
                act.wait_ge(s["ld_a%d" % hf], 32 * (b + 1))
                nc.scalar.activation(s_t[:, hf], s_t[:, hf], ACT.Ln).then_inc(s["inv"], 1)
                act.wait_ge(s["inv"], 2 * g + 1)
                nc.scalar.activation(s_t[:, hf], s_t[:, hf], ACT.Exp, scale=-1.0).then_inc(s["inv"], 1)

            chunks(act, sigmoid)

        @block.gpsimd
        def _(pool):
            def add(b, hf):
                g = b * 2 + hf
                pool.wait_ge(s["sum"], g + 1)
                pool.wait_ge(s["ld_r%d" % hf], 16 * (b + 1))
                nc.gpsimd.tensor_tensor(acc[:, hf], m["x_all"][:, bass.ds(4 * g, 4), :], r_r[:, hf], ALU.add).then_inc(s["add"], 1)

            chunks(pool, add)

        @block.tensor
        def _(pe):
            pe.wait_ge(s["ld_w"], 48)

            def gates(b, hf):
                g = b * 2 + hf
                pe.wait_ge(s["hs"], 2 * g + 2)
                nc.tensor.matmul(psg[0:F, hf], w_sgu[:, 0:F], m["xT_all"][:, bass.ds(g * CH, CH)], start=True, stop=True)
                nc.tensor.matmul(psu[0:F, hf], w_sgu[:, F:2 * F], m["xT_all"][:, bass.ds(g * CH, CH)], start=True, stop=True).then_inc(s["gu"], 1)

            def rows(b, hf):
                g = b * 2 + hf
                pe.wait_ge(s["hs"], 4 + 2 * g + 2)
                pe.wait_ge(s["norm"], g + 1)
                pe.wait_ge(s["sum"], g + 1)
                for i in range(4):
                    o = psy[:, hf, i * P:(i + 1) * P]
                    nc.tensor.matmul(o, a_n[:, hf, i * P:(i + 1) * P], w_o[:], start=True, stop=False)
                    last = nc.tensor.matmul(o, h_t[:, hf, i * P:(i + 1) * P], w_sdn[:], start=False, stop=True)
                last.then_inc(s["y"], 1)

            gates(0, 0)
            with pe.Fori(0, B - 1) as b:
                gates(b, 1)
                rows(b, 0)
                gates(b + 1, 0)
                rows(b, 1)
            gates(B - 1, 1)
            rows(B - 1, 0)
            rows(B - 1, 1)

        @block.vector
        def _(dve):
            dve.sem_inc(s["hs"], 4)
            dve.sem_inc(s["sum"], 2)
            for hf in range(2):
                dve.sem_inc(s["stored%d" % hf], 16)
            nc.vector.memset(one[:], 1.0).then_inc(s["one"], 1)

            def hidden(b, hf):
                g = b * 2 + hf
                dve.wait_ge(s["ex"], 3 * g + 3)
                if not isinstance(g, int) or g > 1:
                    dve.wait_ge(s["y"], g - 1)
                nc.vector.tensor_tensor(h_t[:, hf], psg[0:F, hf], sg1[:, hf], ALU.mult).then_inc(s["hs"], 1)
                dve.wait_ge(s["hs"], 4 + 2 * g + 1)
                nc.vector.tensor_tensor(h_t[:, hf], psu[0:F, hf], h_t[:, hf], ALU.mult).then_inc(s["hs"], 1)
                dve.wait_ge(s["inv"], 2 * g + 2)
                nc.vector.tensor_tensor(a_n[:, hf], a_t[:, hf], s_t[:, hf], ALU.mult).then_inc(s["norm"], 1)

            def total(b, hf):
                g = b * 2 + hf
                dve.wait_ge(s["stored%d" % hf], 16 * (b + 1))
                dve.wait_ge(s["add"], g + 1)
                dve.wait_ge(s["y"], g + 1)
                nc.vector.tensor_tensor(res[:, hf], psy[:, hf].rearrange("p (n d) -> p n d", n=4), acc[:, hf],
                                        ALU.add).then_inc(s["sum"], 1)

            hidden(0, 0)
            hidden(0, 1)
            total(0, 0)
            with dve.Fori(1, B) as b:
                hidden(b, 0)
                total(b - 1, 1)
                hidden(b, 1)
                total(b, 0)
            total(B - 1, 1)


def kernel(L0_attn_x, L0_attn_Wq, L0_attn_Wk, L0_attn_Wv, L0_attn_Wo, L0_attn_alpha, L0_ffn_router_w, L0_ffn_w_gate,
           L0_ffn_w_up, L0_ffn_w_down, L0_ffn_ws_gate_up, L0_ffn_ws_down):
    import concourse.bacc as bacc
    from concourse.bass_utils import run_bass_kernel_spmd

    def a(v):
        return np.ascontiguousarray(np.asarray(v))

    other = np.arange(D) ^ 1
    consts = np.zeros((P, 449), np.float32)
    row, col = np.arange(P)[:, None], np.arange(P)[None, :]
    consts[:, 0:P] = np.eye(P)
    consts[:, 128:256] = np.where(col > row, np.float32(MASK_D), 0)
    consts[:, 256:384] = np.where(row > col, np.float32(MASK_T), 0)
    consts[:, 384:400] = np.where(row // HD == np.arange(16)[None, :], -0.5, 0)
    consts[:, 416:448] = T - (np.arange(TILES)[None, :] * P + row)
    consts[:, 448] = np.arange(P) % SLOTS
    freq = np.outer(1.0 / 10000.0 ** (np.arange(0, HD, 2)[:HD // 2] / HD), np.arange(S))
    pair = (np.arange(P) % HD) // 2
    sign = np.where(np.arange(P) % 2 == 0, -1.0, 1.0)[:, None]
    rope = np.stack([np.cos(freq)[pair], sign * np.sin(freq)[pair]], 1).astype(np.float32)

    x = a(L0_attn_x).reshape(T, D)
    wq, wk = a(L0_attn_Wq), a(L0_attn_Wk)
    ins = {
        "x": x, "wq": wq, "wqs": a(wq[:, other]), "wk": wk, "wks": a(wk[:, other]), "wv": a(L0_attn_Wv),
        "wo": a(L0_attn_Wo), "alpha": a(np.broadcast_to(a(L0_attn_alpha), (P, 1))), "rwt": a(a(L0_ffn_router_w).T),
        "wgu": a(np.concatenate([a(L0_ffn_w_gate), a(L0_ffn_w_up)], 2)), "wdn": a(L0_ffn_w_down),
        "wsgu": a(L0_ffn_ws_gate_up), "wsdn": a(L0_ffn_ws_down), "consts": consts, "rope": a(rope),
    }
    nc = bacc.Bacc("TRN2", target_bir_lowering=False, num_devices=1)
    aps = {n: nc.dram_tensor("in_" + n, list(v.shape), mybir.dt.from_np(v.dtype), kind="ExternalInput").ap()
           for n, v in ins.items()}
    out = nc.dram_tensor("out", [T, D], F32, kind="ExternalOutput").ap()
    program(nc, out=out, **aps)
    r = run_bass_kernel_spmd(nc, [{"in_" + n: v for n, v in ins.items()}], core_ids=[0])
    return r.results[0]["out"].reshape(B, S, D)
```

```python
from contextlib import ExitStack

import numpy as np
import concourse.bass as bass
from concourse import mybir

F32 = mybir.dt.float32
BF16 = mybir.dt.bfloat16
I32 = mybir.dt.int32
ALU = mybir.AluOpType
ACT = mybir.ActivationFunctionType
AXX = mybir.AxisListType.X

P = 128
B, S, D = 4, 1024, 128
T = B * S
H, HD = 16, 8
E, TOPK, F = 64, 8, 96
SLOTS = 64
ATT_EPS = 1e-5
LN_EPS = 1e-5
TILES = T // P
CH = 512
NCH = T // CH
NPART = 3
GH = 4
QT = S // P
TRIPS = B * H // (2 * GH)
PROD = NPART * NPART * HD
NORM_K = PROD
NORM_Q = 96
DUMMY = SLOTS
ROW = D + E
MASK_D = -1e18
MASK_T = -1e30
ACT_SET = "natural_log_exp_and_others"


def ge(eng, sem, value):
    if isinstance(value, int) and value <= 0:
        return
    eng.wait_ge(sem, value)


def wait_apart(eng, sem, value, passed):
    ge(eng, sem, value)
    eng.sem_inc(passed, 1)


def step_list():
    out = []
    for i in reversed(range(QT)):
        w = P * (i + 1)
        n = 1 if w > 512 else 2 if w > 256 else 4
        pitch = w if n != 2 else 512
        out += [(i, list(range(c, c + n)), pitch) for c in range(0, GH, n)]
    return out


STEPS = step_list()
NS = len(STEPS)
NT = 2 * NS
ROUTE = 19
LEAD = 4


def value_work():
    work = [[] for _ in range(NS)]
    for i in range(QT):
        at = [n for n in range(NS) if STEPS[n][0] == (i - 1 if i else 0)]
        for a, n in enumerate(at):
            work[n].append((i, (i + 1) * a // len(at), (i + 1) * (a + 1) // len(at)))
    return [sorted(w, reverse=True) for w in work]


VALUES = value_work()
HALF_END = [max(n for n in range(NS) if any(w[0] == i for w in VALUES[n])) for i in (QT // 2, 0)]


def program(nc, x, wq, wqs, wk, wks, wv, wo, alpha, rwt, wgu, wdn, wsgu, wsdn, consts, rope, out):
    with ExitStack() as ctx:
        def sb(name, shape, dt=F32, c=ctx):
            return c.enter_context(nc.sbuf_tensor(name, shape, dt))

        def ps(name, shape, c):
            return c.enter_context(nc.psum_tensor(name, shape, F32))

        def sem(name, c=ctx):
            return c.enter_context(nc.semaphore(name))

        qk_parts = nc.dram_tensor("qk_parts", [B, 2, H, NPART * HD, S], BF16, kind="Internal").ap()
        nrm_parts = nc.dram_tensor("nrm_parts", [B, 2, NPART, H, S], BF16, kind="Internal").ap()
        rows = nc.dram_tensor("rows", [T + DUMMY, ROW], F32, kind="Internal").ap()
        routed = nc.dram_tensor("routed", [T + DUMMY, D], F32, kind="Internal").ap()
        sums_d = nc.dram_tensor("sums_d", [TRIPS, 2, GH, S], F32, kind="Internal").ap()
        att_d = nc.dram_tensor("att_d", [TRIPS, 2, GH * HD, S], F32, kind="Internal").ap()

        x_all = sb("x_all", [P, TILES, D])
        xT_all = sb("xT_all", [P, T])
        w_o = sb("w_o", [P, D])
        w_sgu = sb("w_sgu", [P, 2 * F])
        w_sdn = sb("w_sdn", [F, D])
        ident = sb("ident", [P, P])
        identb = sb("identb", [P, P], BF16)
        mask_d = sb("mask_d", [P, P], BF16)
        mask_t = sb("mask_t", [P, P], BF16)
        cst = sb("cst", [P, consts.shape[1]])
        scale = sb("scale", [P, 1])
        v_all = sb("v_all", [P, TRIPS, QT, 64])
        idx64 = sb("idx64", [SLOTS, E], I32)
        idxp = sb("idxp", [P, E // 2], I32)
        q_d = sb("q_d", [P, 2, GH, S], BF16)
        q_s = sb("q_s", [P, 2, GH, S], BF16)
        k_t = sb("k_t", [P, 2, GH, S], BF16)
        ld0, ld1 = sem("ld_qk0"), sem("ld_qk1")
        o_stored0, o_stored1 = sem("o_stored0"), sem("o_stored1")
        C_MD, C_MT, C_NB, C_TV, C_SI = 128, 256, 384, 416, 448

        shared = dict(w_o=w_o, w_sgu=w_sgu, w_sdn=w_sdn,
                      ld0=ld0, ld1=ld1, o_stored0=o_stored0, o_stored1=o_stored1,
                      ident=ident, identb=identb, q_d=q_d, q_s=q_s, k_t=k_t,
                      mask_d=mask_d, mask_t=mask_t, scale=scale, v_all=v_all, idx64=idx64,
                      idxp=idxp, qk_parts=qk_parts, nrm_parts=nrm_parts, rows=rows, routed=routed,
                      xT_all=xT_all, x_all=x_all, att_d=att_d, sums_d=sums_d)
        with ExitStack() as pc:
            w_q = sb("w_q", [P, D], F32, pc)
            w_qs = sb("w_qs", [P, D], F32, pc)
            w_k = sb("w_k", [P, D], F32, pc)
            w_ks = sb("w_ks", [P, D], F32, pc)
            w_v = sb("w_v", [P, D], F32, pc)
            w_r = sb("w_r", [P, E], F32, pc)
            tabs = sb("tabs", [P, 2, S], F32, pc)
            zero = sb("zero", [P, 13 * D], F32, pc)
            st6 = sb("st6", [P, TILES, 6], F32, pc)
            mv = sb("mv", [P, TILES, 2], F32, pc)
            rstd = sb("rstd", [P, TILES], F32, pc)
            al = sb("al", [P, 1], F32, pc)
            xn = sb("xn", [P, 2, 4, D], F32, pc)
            xT = sb("xT", [P, 2, CH], F32, pc)
            xs = sb("xs", [P, 2, CH], F32, pc)
            best = sb("best", [P, 8], F32, pc)
            ra = sb("ra", [P, 2, CH], F32, pc)
            rb = sb("rb", [P, 2, CH], F32, pc)
            qf = sb("qf", [P, 2, CH], F32, pc)
            res = sb("res", [P, 2, CH], F32, pc)
            sq = sb("sq", [P, 2, CH], F32, pc)
            parts = sb("parts", [P, 2, 2, NPART, CH], BF16, pc)
            nf = sb("nf", [64, CH], F32, pc)
            nres = sb("nres", [64, CH], F32, pc)
            nparts = sb("nparts", [64, 2, NPART, CH], BF16, pc)
            nmax = sb("nmax", [P, 4], F32, pc)
            pe_ = sb("pexp", [P, 2, 4, E], F32, pc)
            top8 = sb("top8", [P, 4, 8], F32, pc)
            mr = sb("mr", [P, 4, E], F32, pc)
            sel = sb("sel", [P, 4, E], F32, pc)
            wsum = sb("wsum", [P, 4], F32, pc)
            rws = sb("rws", [P, 4], F32, pc)
            wts = sb("wts", [P, 2, 4, E], F32, pc)
            selv = sb("selv", [P, 2, 2, 2, E], F32, pc)
            selT = sb("selT", [P, T // 2], F32, pc)
            cand = sb("cand", [P, SLOTS], F32, pc)
            both = sb("both", [E, 2 * SLOTS], F32, pc)
            topv = sb("topv", [E, SLOTS], F32, pc)
            emp = sb("emp", [SLOTS, E], F32, pc)
            tok = sb("tok", [SLOTS, E], F32, pc)

            with ExitStack() as pp:
                psT = ps("psT", [P, CH], pp)
                psL = ps("psL", [P, CH], pp)
                psV = ps("psV", [P, CH], pp)
                psQ = ps("psQ", [P, 4, CH], pp)
                psN = ps("psN", [P, CH], pp)
                names = ("ld_w ld_out ld_c ld_rope consts_cast stat seps lnv rstd_ready zeroed zero_out scl xn_ready "
                         "xT_ps xT_ready xs_ready lg_ps q_ps k_ps v_ps v_out turned cast resid n_ps n_ready n_cast n_resid "
                         "nmax_ready pexp routing selT_ps selT_ready st_xn0 st_xn1 st_xT0 st_xT1 st_parts0 st_parts1 "
                         "st_nrm0 st_nrm1 st_w0 st_w1 dve_passed sp_passed found tv_ps").split()
                s = {n: sem(n, pp) for n in names}
                XG = 4
                ld_x = [sem("ld_x%d" % i, pp) for i in range(XG)]
                block = pp.enter_context(nc.Block())
                xv = x.rearrange("(n p) d -> p n d", p=P)
                STORES = (("xn", 1), ("xT", 1), ("parts", 2 * NPART), ("w", 1), ("nrm", 2))

                def rows_pass(eng, iteration):
                    iteration((0, 0), None, None)
                    iteration((0, 1), (0, 0), None)
                    iteration((1, 0), (0, 1), (0, 0))
                    with eng.Fori(1, B - 1) as b:
                        iteration((b, 1), (b, 0), (b - 1, 1))
                        iteration((b + 1, 0), (b, 1), (b, 0))
                    iteration((B - 1, 1), (B - 1, 0), (B - 2, 1))
                    iteration(None, (B - 1, 1), (B - 1, 0))
                    iteration(None, None, (B - 1, 1))

                def heads_pass(eng, iteration):
                    iteration((0, 0), None)
                    with eng.Fori(0, B - 1) as b:
                        iteration((b, 1), (b, 0))
                        iteration((b + 1, 0), (b, 1))
                    iteration((B - 1, 1), (B - 1, 0))
                    iteration(None, (B - 1, 1))

                def following(b, hf):
                    if isinstance(b, int) and b * 2 + hf == NCH - 1:
                        return None
                    return (b + hf, 1 - hf)

                @block.sync
                def _(sp):
                    n = TILES // XG
                    sp.dma_start(x_all[:, 0:n, :], xv[:, 0:n, :]).then_inc(ld_x[0], 16)
                    sp.dma_start(cst[:], consts).then_inc(s["ld_c"], 16)
                    for g in range(1, XG):
                        sp.dma_start(x_all[:, g * n:(g + 1) * n, :], xv[:, g * n:(g + 1) * n, :]).then_inc(ld_x[g], 16)
                    for dst, src in ((w_o, wo), (w_sgu, wsgu), (w_sdn, wsdn)):
                        sp.dma_start(dst[:], src).then_inc(s["ld_out"], 16)
                    sp.wait_ge(s["zeroed"], 1)
                    sp.dma_start(rows[T:T + DUMMY, :], zero[0:DUMMY, 0:ROW]).then_inc(s["zero_out"], 16)
                    step = 13
                    for r in range(0, T + DUMMY, step * P):
                        k = min(step, (T + DUMMY - r) // P)
                        if k:
                            sp.dma_start(routed[r:r + k * P, :].rearrange("(p n) d -> p (n d)", p=P),
                                         zero[:, 0:k * D]).then_inc(s["zero_out"], 16)
                    done = (T + DUMMY) // P * P
                    sp.dma_start(routed[done:T + DUMMY, :], zero[0:T + DUMMY - done, 0:D]).then_inc(s["zero_out"], 16)
                    nz = 2 + -(-(done // P) // step)

                    def stage(b, hf):
                        g = b * 2 + hf
                        sp.wait_ge(s["xn_ready"], g * 4 + 4)
                        sp.dma_start(rows[bass.ds(g * CH, CH), 0:D].rearrange("(n p) d -> p n d", p=P),
                                     xn[:, hf]).then_inc(s["st_xn%d" % hf], 16)
                        wait_apart(sp, s["xT_ready"], g + 2, s["sp_passed"])
                        sp.dma_start(xT_all[:, bass.ds(g * CH, CH)], xT[:, hf]).then_inc(s["st_xT%d" % hf], 16)

                    def routed_out(b, hf):
                        g = b * 2 + hf
                        wait_apart(sp, s["routing"], g * ROUTE + ROUTE, s["sp_passed"])
                        sp.dma_start(rows[bass.ds(g * CH, CH), D:ROW].rearrange("(n p) d -> p n d", p=P),
                                     wts[:, hf]).then_inc(s["st_w%d" % hf], 16)

                    def rows_iteration(cur, prev, prev2):
                        if cur:
                            stage(*cur)
                        if prev:
                            routed_out(*prev)

                    def first_load():
                        for hf in range(2):
                            sp.wait_ge(s["st_parts%d" % hf], 16 * 2 * NPART * 2)
                            sp.wait_ge(s["st_nrm%d" % hf], 32 * 2)
                        sp.wait_ge(s["zeroed"], 5)
                        load_group(sp, shared, ld0, 0, 0, 0)

                    def heads_iteration(cur, prev):
                        if not prev:
                            return
                        b, hf = prev
                        if isinstance(b, int) and (b, hf) == (B - 1, 0):
                            first_load()
                        g = b * 2 + hf
                        wait_apart(sp, s["resid"], 4 + g * 4 + 4, s["sp_passed"])
                        for w in range(2):
                            for part in range(NPART):
                                dst = qk_parts[bass.ds(b, 1), w, :, part * HD:(part + 1) * HD, hf * CH:(hf + 1) * CH]
                                sp.dma_start(dst.rearrange("o h d s -> (o h) d s"),
                                             parts[:, hf, w, part, :]).then_inc(s["st_parts%d" % hf], 16)
                        wait_apart(sp, s["n_resid"], 2 + g * 2 + 2, s["sp_passed"])
                        for w in range(2):
                            dst = nrm_parts[bass.ds(b, 1), w, :, :, hf * CH:(hf + 1) * CH]
                            sp.dma_start(dst.rearrange("o a h s -> h (o a) s"),
                                         nparts[32 * w:32 * w + H, hf]).then_inc(s["st_nrm%d" % hf], 16)

                    rows_pass(sp, rows_iteration)
                    heads_pass(sp, heads_iteration)
                    sp.wait_ge(s["ld_out"], 48)
                    sp.wait_ge(s["zero_out"], 16 * nz)
                    for hf in range(2):
                        for name, dmas in STORES:
                            sp.wait_ge(s["st_%s%d" % (name, hf)], 16 * dmas * (B + 1))

                @block.gpsimd
                def _(pool):
                    nc.gpsimd.memset(zero[:], 0.0).then_inc(s["zeroed"], 1)

                    for at, (buf, value) in enumerate(((q_d, 1.0), (q_s, 0.0), (k_t, 0.0))):
                        pool.wait_ge(s["zeroed"], at + 1)
                        nc.gpsimd.memset(buf[64:P], value).then_inc(s["zeroed"], 1)
                    pool.wait_ge(s["zeroed"], 4)
                    nc.gpsimd.memset(k_t[NORM_Q:NORM_Q + NPART], 1.0).then_inc(s["zeroed"], 1)
                    pool.wait_ge(s["zeroed"], 5)

                    def second(b, hf, w):
                        pool.wait_ge(s["cast"], 6 + (b * 2 + hf) * 6 + 3 * w + 1)
                        nc.gpsimd.tensor_tensor(res[:, w], qf[:, w], parts[:, hf, w, 0, :], ALU.subtract).then_inc(s["resid"], 1)

                    def third(b, hf, w):
                        pool.wait_ge(s["cast"], 6 + (b * 2 + hf) * 6 + 3 * w + 3)
                        nc.gpsimd.tensor_tensor(parts[:, hf, w, 2, :], res[:, w], parts[:, hf, w, 1, :],
                                                ALU.subtract).then_inc(s["resid"], 1)

                    def settled(done, n_done):
                        pool.wait_ge(s["resid"], done)
                        ge(pool, s["n_resid"], n_done)

                    def iteration(cur, prev):
                        if prev:
                            third(*prev, 1)
                            gp_ = prev[0] * 2 + prev[1]
                        if cur:
                            second(*cur, 0)
                            g = cur[0] * 2 + cur[1]
                        if prev:
                            settled(4 + gp_ * 4 + 4 + (1 if cur else 0), gp_ * 2 + 2)
                            pool.wait_ge(s["n_cast"], gp_ * 2 + 1)
                            nc.gpsimd.tensor_tensor(nres[:], nf[:], nparts[:, prev[1], 0, :], ALU.subtract).then_inc(s["n_resid"], 1)
                        if cur:
                            if prev:
                                settled(4 + g * 4 + 1, 2 + gp_ * 2 + 1)
                            third(*cur, 0)
                            second(*cur, 1)
                        if prev:
                            settled(4 + gp_ * 4 + 4 + (3 if cur else 0), 2 + gp_ * 2 + 1)
                            pool.wait_ge(s["n_cast"], gp_ * 2 + 2)
                            nc.gpsimd.tensor_tensor(nparts[:, prev[1], 2, :], nres[:], nparts[:, prev[1], 1, :],
                                                    ALU.subtract).then_inc(s["n_resid"], 1)
                            if cur:
                                settled(4 + g * 4 + 3, 2 + gp_ * 2 + 2)

                    heads_pass(pool, iteration)

                @block.scalar
                def _(act):
                    for dst, src in ((w_r, rwt), (w_q, wq), (w_qs, wqs), (w_k, wk), (w_ks, wks), (w_v, wv), (al, alpha)):
                        act.dma_start(dst[:], src).then_inc(s["ld_w"], 16)
                    act.dma_start(tabs[:], rope).then_inc(s["ld_rope"], 16)
                    act.sem_inc(s["xT_ready"], 1)
                    act.sem_inc(s["pexp"], 4)
                    act.sem_inc(s["v_out"], 1)
                    act.sem_inc(s["v_ps"], 2)
                    act.sem_inc(s["cast"], 6)
                    act.sem_inc(s["selT_ready"], 2)
                    for hf in range(2):
                        for name, dmas in STORES:
                            act.sem_inc(s["st_%s%d" % (name, hf)], 16 * dmas)
                    nc.scalar.preload_act_table_set(ACT_SET)

                    def inverse_deviation(at, part):
                        act.wait_ge(s["seps"], at + 1)
                        nc.scalar.activation(part, part, ACT.Ln).then_inc(s["lnv"], 1)
                        act.wait_ge(s["lnv"], at + 1)
                        nc.scalar.activation(part, part, ACT.Exp, scale=-0.5).then_inc(s["rstd_ready"], 1)


                    def rows_out(b, hf):
                        g = b * 2 + hf
                        act.wait_ge(s["st_xT%d" % hf], 16 * (b + 1))
                        act.wait_ge(s["xT_ps"], g + 1)
                        nc.scalar.activation(xT[:, hf], psT[:], ACT.Copy).then_inc(s["xT_ready"], 1)

                    def routing(b, hf):
                        ge(act, s["routing"], (b * 2 + hf - 1) * ROUTE)
                        act.wait_ge(s["nmax_ready"], b * 2 + hf + 1)
                        for i in range(4):
                            nc.scalar.activation(pe_[:, hf, i, :], psL[:, i * E:(i + 1) * E], ACT.Exp,
                                                 bias=nmax[:, i:i + 1]).then_inc(s["pexp"], 1)

                    def selected(b, hf):
                        g = b * 2 + hf
                        act.wait_ge(s["selT_ps"], g + 1)
                        nc.scalar.activation(selT[:, bass.ds(g * 256, 256)], psN[:, 0:256], ACT.Copy).then_inc(s["selT_ready"], 1)

                    def first(b, hf, w):
                        act.wait_ge(s["st_parts%d" % hf], 16 * 2 * NPART * (b + 1))
                        act.wait_ge(s["turned"], 6 + (b * 2 + hf) * 6 + 3 * w + 3)
                        nc.scalar.activation(parts[:, hf, w, 0, :], qf[:, w], ACT.Copy).then_inc(s["cast"], 1)
                        ge(act, s["n_ps"], b * 2 + hf)
                        nc.scalar.activation(sq[:, w], qf[:, w], ACT.Square).then_inc(s["cast"], 1)

                    def second(b, hf, w):
                        act.wait_ge(s["resid"], 4 + (b * 2 + hf) * 4 + 2 * w + 1)
                        nc.scalar.activation(parts[:, hf, w, 1, :], res[:, w], ACT.Copy).then_inc(s["cast"], 1)

                    def values(b, hf):
                        act.wait_ge(s["v_ps"], b * 2 + hf + 3)
                        dst = v_all[:, bass.ds(b * 2, 2), 4 * hf:4 * hf + 4, :]
                        nc.scalar.activation(dst, psV[:].rearrange("p (i g c) -> p g i c", i=4, g=2),
                                             ACT.Copy).then_inc(s["v_out"], 1)

                    def norm_first(b, hf):
                        act.wait_ge(s["st_nrm%d" % hf], 32 * (b + 1))
                        act.wait_ge(s["n_ready"], b * 2 + hf + 2)
                        nc.scalar.activation(nparts[:, hf, 0, :], nf[:], ACT.Copy).then_inc(s["n_cast"], 1)

                    def norm_second(b, hf):
                        act.wait_ge(s["n_resid"], 2 + (b * 2 + hf) * 2 + 1)
                        nc.scalar.activation(nparts[:, hf, 1, :], nres[:], ACT.Copy).then_inc(s["n_cast"], 1)

                    def again(b, hf):
                        g = b * 2 + hf
                        act.wait_ge(s["v_ps"], g + 1)
                        nc.scalar.activation(xs[:, hf], xT_all[:, bass.ds(g * CH, CH)], ACT.Copy).then_inc(s["xs_ready"], 1)

                    def rows_iteration(cur, prev, prev2):
                        if cur:
                            rows_out(*cur)
                        if cur and not prev:
                            inverse_deviation(1, rstd[:, TILES // XG:])
                        if cur:
                            routing(*cur)
                        if prev and not cur:
                            act.wait_ge(s["st_xT0"], 16 * (B + 1))
                            again(0, 0)
                        if prev2:
                            selected(*prev2)

                    def heads_iteration(cur, prev):
                        if prev:
                            second(*prev, 1)
                        if cur:
                            first(*cur, 0)
                        if cur and following(*cur):
                            again(*following(*cur))
                        if prev:
                            norm_first(*prev)
                        if cur:
                            second(*cur, 0)
                            first(*cur, 1)
                        if prev:
                            norm_second(*prev)
                        if cur:
                            values(*cur)

                    inverse_deviation(0, rstd[:, 0:TILES // XG])
                    rows_pass(act, rows_iteration)
                    act.wait_ge(s["st_xT1"], 16 * (B + 1))
                    heads_pass(act, heads_iteration)
                    act.wait_ge(s["ld_w"], 16 * 7)
                    nc.scalar.activation(scale[:], al[:], ACT.Exp,
                                         scale=float(np.log(np.sqrt(np.float32(HD)) / np.log(np.float32(1 + HD))))
                                         ).then_inc(s["scl"], 1)

                @block.tensor
                def _(pe):
                    pe.wait_ge(s["ld_c"], 16)
                    pe.wait_ge(s["ld_w"], 16 * 7)

                    def norms(b, hf):
                        g = b * 2 + hf
                        pe.wait_ge(s["cast"], 6 + g * 6 + 5)
                        pe.wait_ge(s["n_ready"], g + 1)
                        for w in range(2):
                            last = nc.tensor.matmul(psN[32 * w:32 * w + 32, :], cst[:, C_NB:C_NB + 32], sq[:, w],
                                                    start=True, stop=True)
                        last.then_inc(s["n_ps"], 1)

                    def turn_selected(b, hf):
                        g = b * 2 + hf
                        pe.wait_ge(s["routing"], g * ROUTE + ROUTE)
                        pe.wait_ge(s["selT_ready"], g + 2)
                        for j in range(2):
                            last = nc.tensor.transpose(psN[:, j * P:(j + 1) * P],
                                                       selv[:, hf, j].rearrange("p a e -> p (a e)"), cst[:, 0:P])
                        last.then_inc(s["selT_ps"], 1)

                    def values(b, hf):
                        g = b * 2 + hf
                        pe.wait_ge(s["v_out"], g + 1)
                        for i in range(4):
                            last = nc.tensor.matmul(psV[:, i * P:(i + 1) * P], xs[:, hf, i * P:(i + 1) * P], w_v[:],
                                                    start=True, stop=True)
                        last.then_inc(s["v_ps"], 1)

                    def logits(b, hf):
                        g = b * 2 + hf
                        pe.wait_ge(s["xn_ready"], g * 4 + 4)
                        pe.wait_ge(s["xT_ready"], g + 1)
                        for i in range(4):
                            last = nc.tensor.transpose(psT[:, i * P:(i + 1) * P], xn[:, hf, i, :], cst[:, 0:P])
                        last.then_inc(s["xT_ps"], 1)
                        pe.wait_ge(s["xT_ready"], g + 2)
                        pe.wait_ge(s["pexp"], g * 4 + 4)
                        for i in range(4):
                            last = nc.tensor.matmul(psL[:, i * E:(i + 1) * E], xT[:, hf, i * P:(i + 1) * P], w_r[:],
                                                    start=True, stop=True)
                        last.then_inc(s["lg_ps"], 1)

                    def heads(b, hf, w):
                        g = b * 2 + hf
                        wa, wb = ((w_q, w_qs), (w_k, w_ks))[w]
                        pe.wait_ge(s["turned"], g * 6 + 3 * w + 2)
                        nc.tensor.matmul(psQ[:, 2 * w, :], wa[:], xs[:, hf], start=True, stop=True)
                        nc.tensor.matmul(psQ[:, 2 * w + 1, :], wb[:], xs[:, hf], start=True, stop=True)\
                            .then_inc(s["k_ps" if w else "q_ps"], 1)

                    def rows_iteration(cur, prev, prev2):
                        if cur:
                            logits(*cur)
                        if not cur and not prev:
                            pe.wait_ge(s["xs_ready"], 1)
                            heads(0, 0, 0)
                        if prev2:
                            turn_selected(*prev2)

                    def heads_iteration(cur, prev):
                        if cur:
                            if prev:
                                pe.wait_ge(s["xs_ready"], cur[0] * 2 + cur[1] + 1)
                                heads(*cur, 0)
                        if prev:
                            norms(*prev)
                        if cur:
                            heads(*cur, 1)
                            values(*cur)

                    rows_pass(pe, rows_iteration)
                    pe.wait_ge(s["selT_ready"], NCH + 2)
                    heads_pass(pe, heads_iteration)
                    pe.wait_ge(s["found"], 3 * NCH + 2 + 2 * (SLOTS // 8))
                    nc.tensor.transpose(psT[0:SLOTS, 0:E], topv[:], cst[0:E, 0:E]).then_inc(s["tv_ps"], 1)

                @block.vector
                def _(dve):
                    dve.sem_inc(s["turned"], 6)
                    dve.sem_inc(s["resid"], 4)
                    dve.sem_inc(s["n_ready"], 1)
                    dve.sem_inc(s["n_resid"], 2)
                    dve.wait_ge(s["ld_c"], 16)
                    for dst, c0 in ((identb, 0), (mask_d, C_MD), (mask_t, C_MT), (ident, 0)):
                        nc.vector.tensor_copy(dst[:], cst[:, c0:c0 + P]).then_inc(s["consts_cast"], 1)

                    def statistics(groups):
                        per = TILES // XG
                        for a in groups:
                            dve.wait_ge(ld_x[a], 16)
                            for n in range(a * per, (a + 1) * per):
                                nc.vector.bn_stats(st6[:, n, :], x_all[:, n, :]).then_inc(s["stat"], 1)
                        t0, t1 = groups[0] * per, groups[-1] * per + per
                        dve.wait_ge(s["stat"], t0 + t1)
                        for n in range(t0, t1):
                            nc.vector.bn_aggr(mv[:, n, :], st6[:, n, :]).then_inc(s["stat"], 1)
                        dve.wait_ge(s["stat"], 2 * t1)
                        nc.vector.tensor_scalar(rstd[:, t0:t1], mv[:, t0:t1, 1], LN_EPS, None, ALU.add).then_inc(s["seps"], 1)

                    def normalise(b, hf):
                        g = b * 2 + hf
                        dve.wait_ge(s["st_xn%d" % hf], 16 * (b + 1))
                        if not isinstance(g, int):
                            dve.wait_ge(s["xT_ps"], g - 1)
                        elif g >= 2:
                            dve.wait_ge(s["xT_ps"], g - 1)
                        for i in range(4):
                            n = g * 4 + i
                            nc.vector.tensor_scalar(xn[:, hf, i, :], x_all[:, bass.ds(n, 1), :].rearrange("p o d -> p (o d)"),
                                                    mv[:, bass.ds(n, 1), 0], rstd[:, bass.ds(n, 1)],
                                                    ALU.subtract, ALU.mult).then_inc(s["xn_ready"], 1)

                    def maxima(b, hf):
                        g = b * 2 + hf
                        dve.wait_ge(s["lg_ps"], g + 1)
                        dve.wait_ge(s["pexp"], g * 4 + 4)
                        nc.vector.tensor_reduce(nmax[:], psL[:, 0:256].rearrange("p (i e) -> p i e", i=4), AXX, ALU.max,
                                                negate=True).then_inc(s["nmax_ready"], 1)

                    def turn(b, hf, w):
                        g = b * 2 + hf
                        dve.wait_ge(s["k_ps" if w else "q_ps"], g + 1)
                        nc.vector.tensor_tensor(ra[:, w], psQ[:, 2 * w, :], tabs[:, 0, hf * CH:(hf + 1) * CH],
                                                ALU.mult).then_inc(s["turned"], 1)
                        nc.vector.tensor_tensor(rb[:, w], psQ[:, 2 * w + 1, :], tabs[:, 1, hf * CH:(hf + 1) * CH],
                                                ALU.mult).then_inc(s["turned"], 1)
                        dve.wait_ge(s["turned"], 6 + g * 6 + 3 * w + 2)
                        dve.wait_ge(s["cast"], g * 6 + 3 * w + 2)
                        dve.wait_ge(s["resid"], g * 4 + 2 * w + 1)
                        nc.vector.tensor_tensor(qf[:, w], ra[:, w], rb[:, w], ALU.add).then_inc(s["turned"], 1)

                    def after(b, hf):
                        g = b * 2 + hf
                        count = [0]

                        def mark(ins):
                            ins.then_inc(s["routing"], 1)
                            count[0] += 1

                        def settled():
                            wait_apart(dve, s["routing"], g * ROUTE + count[0], s["dve_passed"])
                        wait_apart(dve, s["pexp"], g * 4 + 8, s["dve_passed"])
                        for i in range(4):
                            mark(nc.vector.max(top8[:, i, :], pe_[:, hf, i, :]))
                        settled()
                        for i in range(4):
                            mark(nc.vector.match_replace(mr[:, i, :], top8[:, i, :], pe_[:, hf, i, :], -1.0))
                        mark(nc.vector.reduce_sum(wsum[:], top8[:], AXX))
                        settled()
                        mark(nc.vector.tensor_scalar(sel[:], mr[:], 0.0, None, ALU.is_lt))
                        mark(nc.vector.reciprocal(rws[:], wsum[:]))
                        dve.wait_ge(s["selT_ready"], g + 1)
                        settled()
                        for i in range(4):
                            mark(nc.vector.tensor_scalar(selv[:, hf, i % 2, i // 2, :], sel[:, i, :],
                                                         cst[:, bass.ds(C_TV + g * 4 + i, 1)], None, ALU.mult))
                        dve.wait_ge(s["st_w%d" % hf], 16 * (b + 1))
                        for i in range(4):
                            mark(nc.vector.scalar_tensor_tensor(wts[:, hf, i, :], pe_[:, hf, i, :], rws[:, i:i + 1], sel[:, i, :],
                                                                ALU.mult, ALU.mult))
                        assert count[0] == ROUTE

                    def norm(b, hf):
                        g = b * 2 + hf
                        dve.wait_ge(s["n_ps"], g + 1)
                        dve.wait_ge(s["n_resid"], g * 2 + 1)
                        nc.vector.tensor_scalar(nf[:], psN[0:64, :], -0.25 * ATT_EPS, None, ALU.add).then_inc(s["n_ready"], 1)

                    statistics([0])
                    dve.wait_ge(s["rstd_ready"], 1)
                    normalise(0, 0)
                    statistics(list(range(1, XG)))
                    dve.wait_ge(s["rstd_ready"], 2)
                    dve.wait_ge(s["ld_rope"], 16)

                    def rows_iteration(cur, prev, prev2):
                        if cur:
                            maxima(*cur)
                            if following(*cur):
                                normalise(*following(*cur))
                        if prev:
                            after(*prev)

                    assert SLOTS // 8 == NCH

                    def candidates(b, hf):
                        g = b * 2 + hf
                        if not isinstance(g, int) or g:
                            wait_apart(dve, s["found"], 3 * g, s["dve_passed"])
                        nc.vector.max(best[:], selT[:]).then_inc(s["found"], 1)
                        wait_apart(dve, s["found"], 3 * g + 1, s["dve_passed"])
                        nc.vector.match_replace(selT[:], best[:], selT[:], 0.0).then_inc(s["found"], 1)
                        nc.vector.tensor_copy(cand[:, bass.ds(8 * g, 8)], best[:]).then_inc(s["found"], 1)

                    def heads_iteration(cur, prev):
                        if cur:
                            turn(*cur, 0)
                        if prev:
                            norm(*prev)
                        if cur:
                            turn(*cur, 1)
                            candidates(*cur)

                    rows_pass(dve, rows_iteration)
                    dve.wait_ge(s["selT_ready"], NCH + 2)
                    heads_pass(dve, heads_iteration)

                    n = 3 * NCH

                    def done(ins):
                        nonlocal n
                        n += 1
                        ins.then_inc(s["found"], 1)
                        dve.wait_ge(s["found"], n)

                    dve.wait_ge(s["found"], n)
                    done(nc.vector.tensor_copy(both[:, 0:SLOTS], cand[0:E, :]))
                    done(nc.vector.tensor_copy(both[:, SLOTS:2 * SLOTS], cand[E:P, :]))
                    for r in range(SLOTS // 8):
                        m = topv[:, 8 * r:8 * r + 8]
                        done(nc.vector.max(m, both[:]))
                        done(nc.vector.match_replace(both[:], m, both[:], 0.0))
                    dve.wait_ge(s["tv_ps"], 1)
                    done(nc.vector.tensor_scalar(emp[:], psT[0:SLOTS, 0:E], 0.0, cst[0:SLOTS, C_SI:C_SI + 1],
                                                 ALU.is_equal, ALU.mult))
                    done(nc.vector.tensor_scalar(tok[:], psT[0:SLOTS, 0:E], -1.0, float(T), ALU.mult, ALU.add))
                    done(nc.vector.tensor_tensor(tok[:], tok[:], emp[:], ALU.add))
                    done(nc.vector.tensor_copy(idx64[:], tok[:]))
                    pairs = tok[:].rearrange("c (r o) -> c o r", o=2)
                    done(nc.vector.tensor_copy(idxp[0:SLOTS, :], pairs[:, 0, :]))
                    done(nc.vector.tensor_copy(idxp[SLOTS:P, :], pairs[:, 1, :]))

        attend(nc, shared, wgu, wdn)
        output(nc, shared, out)



def load_group(sp, m, ld, b, gp, par):
    q_d, q_s, k_t = m["q_d"], m["q_s"], m["k_t"]
    h0 = 8 * gp + GH * par
    src = m["qk_parts"][bass.ds(b, 1)].rearrange("o w h r s -> (o w) r h s")
    nrm = m["nrm_parts"][bass.ds(b, 1)].rearrange("o w a h s -> (o w) a h s")
    for c in range(NPART):
        r0, r1 = c * NPART * HD, (c + 1) * NPART * HD
        qa = src[0, :, h0:h0 + GH, :]
        sp.dma_start(q_d[r0:r1, par], qa).then_inc(ld, 16)
        sp.dma_start(q_s[r0:r1, par], qa).then_inc(ld, 16)
        for r in range(r0, r1, HD):
            sp.dma_start(k_t[r:r + HD, par], src[1, c * HD:(c + 1) * HD, h0:h0 + GH, :]).then_inc(ld, 16)
    sp.dma_start(q_d[NORM_Q:NORM_Q + NPART, par], nrm[0, :, h0:h0 + GH, :]).then_inc(ld, 16)
    sp.dma_start(k_t[NORM_K:NORM_K + NPART, par], nrm[1, :, h0:h0 + GH, :]).then_inc(ld, 16)


def attend(nc, m, wgu, wdn):
    with ExitStack() as ctx:
        def sb(name, shape, dt=F32):
            return ctx.enter_context(nc.sbuf_tensor(name, shape, dt))

        def ps(name, shape):
            return ctx.enter_context(nc.psum_tensor(name, shape, F32))

        q_d, q_s, k_t = m["q_d"], m["q_s"], m["k_t"]
        v_aug = sb("v_aug", [P, 2, QT, GH, 32])
        r_buf = sb("r_buf", [P, 2, S])
        z_buf = sb("z_buf", [P, 4, S])
        m_buf = sb("m_buf", [P, 8, GH])
        p_buf = sb("p_buf", [P, 2, GH, S])
        one = sb("one", [P, 1])
        o_n = sb("o_n", [P, 2, CH])
        xg = sb("xg", [P, 2, ROW])
        xgT = sb("xgT", [P, P])
        w_gu = sb("w_gu", [P, 2, 2, 2 * F])
        w_dn = sb("w_dn", [F, 2, 2, D])
        h_a = sb("h_a", [P, F])
        h_b = sb("h_b", [P, F])
        hT = sb("hT", [F, P])
        ys = sb("ys", [2 * SLOTS, 2, D])
        gidx = sb("gidx", [P, 2, 1], I32)
        sidx = sb("sidx", [SLOTS, 2, 2], I32)

        ps_d = ps("ps_d", [P, S])
        ps_s = ps("ps_s", [P, S])
        ps_t = ps("ps_t", [P, S])
        ps_o = ps("ps_o", [P, CH])
        ps_m = ps("ps_m", [P, CH])

        names = ("d_ready s_ready ln_done r_ready z_done m_done u_ready t_ready p_done pv_done "
                 "o_out ones v_loaded v_clear ld_w0 ld_w1 x_idx x_got0 x_got1 xT_ps xT_ok gu_ps "
                 "gu_exp h_step hT_ps hT_ok y_ps y_ok sc_idx scat dve_passed sp_passed pool_passed").split()
        s = {n: ctx.enter_context(nc.semaphore("b_" + n)) for n in names}
        s.update(ld0=m["ld0"], ld1=m["ld1"], o_stored0=m["o_stored0"], o_stored1=m["o_stored1"])
        block = ctx.enter_context(nc.Block())
        LOADS = NPART * (2 + NPART) + 2
        PAIR_AT = NT // 4
        PV0, YPS0, YOK0, PD0 = 9, 2, 2, 1

        def seg(buf, step):
            i, heads, pitch = step
            return buf[:, 0:len(heads) * pitch].rearrange("p (c w) -> p c w", c=len(heads))[:, :, 0:P * (i + 1)]

        def unit_of(n):
            return 8 * (n // NS) + (QT - 1 - STEPS[n % NS][0])

        def trips(eng, lead, stages):
            def iteration(t, n, last):
                for ahead, stage in stages:
                    if n + ahead < NT:
                        stage(t, n + ahead)
                    elif not last:
                        stage(t + 1, n + ahead - NT)

            for n in range(-lead, 0):
                for ahead, stage in stages:
                    if n + ahead >= 0:
                        stage(0, n + ahead)
            with eng.Fori(0, TRIPS - 1) as t:
                for n in range(NT):
                    iteration(t, n, False)
            for n in range(NT):
                iteration(TRIPS - 1, n, True)

        @block.sync
        def _(sp):
            def weights(t, p):
                ld = s["ld_w%d" % (p % 2)]
                wait_apart(sp, s["y_ps"], YPS0 + t * 4 + p - 1, s["sp_passed"])
                e0 = t * 8 + 2 * p
                sp.dma_start(w_gu[:, p % 2], wgu[bass.ds(e0, 2)].rearrange("e d f -> d e f")).then_inc(ld, 16)
                sp.dma_start(w_dn[:, p % 2], wdn[bass.ds(e0, 2)].rearrange("e f d -> f e d")).then_inc(ld, 16)

            def store(t, k):
                par, hh = k // 2, k % 2
                wait_apart(sp, s["o_out"], t * 4 + k + 2, s["sp_passed"])
                cols = slice(CH * (1 - hh), CH * (2 - hh))
                for c in range(GH):
                    dst = m["att_d"][bass.ds(t, 1), par, c * HD:(c + 1) * HD, cols].rearrange("o r q -> (o r) q")
                    sp.dma_start(dst, o_n[32 * c:32 * c + HD, hh, :]).then_inc(s["o_stored%d" % hh], 16)
                dst = m["sums_d"][bass.ds(t, 1), par, :, cols].rearrange("o c q -> (o c) q")
                sp.dma_start(dst, o_n[HD:P:32, hh, :]).then_inc(s["o_stored%d" % hh], 16)

            def trip(b, gp, last):
                t = b * 2 + gp
                after = (b, 1) if gp == 0 else (b + 1, 0)
                weights(t, 2)
                store(t, 0)
                if not last:
                    wait_apart(sp, s["s_ready"], t * NT + NS, s["sp_passed"])
                    load_group(sp, m, s["ld0"], *after, 0)
                weights(t, 3)
                store(t, 1)
                if not last:
                    weights(t + 1, 0)
                store(t, 2)
                if not last:
                    wait_apart(sp, s["s_ready"], t * NT + NT, s["sp_passed"])
                    load_group(sp, m, s["ld1"], *after, 1)
                    weights(t + 1, 1)
                store(t, 3)

            weights(0, 0)
            weights(0, 1)
            load_group(sp, m, s["ld1"], 0, 0, 1)
            with sp.Fori(0, B - 1) as b:
                trip(b, 0, False)
                trip(b, 1, False)
            trip(B - 1, 0, False)
            trip(B - 1, 1, True)

        @block.gpsimd
        def _(pool):
            for par in range(2):
                nc.gpsimd.memset(v_aug[:, par], 0.0).then_inc(s["v_clear"], 1)
            pool.wait_ge(s["v_clear"], 2)
            for par in range(2):
                nc.gpsimd.memset(v_aug[:, par, :, :, HD], 1.0).then_inc(s["v_clear"], 1)

            def values(t, par):
                pool.wait_ge(s["pv_done"], PV0 + t * 16 + 8 * par - 8)
                src = m["v_all"][:, bass.ds(t, 1), :, 32 * par:32 * par + 32].rearrange("p o j (c d) -> p (o j) c d", c=GH)
                nc.gpsimd.tensor_copy(v_aug[:, par, :, :, 0:HD], src).then_inc(s["v_loaded"], 1)

            def gather(t, p):
                g = t * 4 + p
                pool.wait_ge(s["y_ok"], YOK0 + g - 1)
                nc.gpsimd.tensor_copy(gidx[:, p % 2], m["idxp"][:, bass.ds(g, 1)]).then_inc(s["x_idx"], 1)
                wait_apart(pool, s["x_idx"], g + 1, s["pool_passed"])
                nc.gpsimd.indirect_dma_start(xg[:, p % 2], None, m["rows"], bass.IndirectOffsetOnAxis(gidx[:, p % 2], 0)
                                             ).then_inc(s["x_got%d" % (p % 2)], 16)

            def added(t, p, e):
                wait_apart(pool, s["scat"], 16 * (2 * (t * 4 + p) + e + 1), s["pool_passed"])

            def scatter(t, p, e):
                g = t * 4 + p
                if e == 0:
                    nc.gpsimd.tensor_copy(sidx[:, p % 2], m["idx64"][:, bass.ds(2 * g, 2)]).then_inc(s["sc_idx"], 1)
                    wait_apart(pool, s["sc_idx"], g + 1, s["pool_passed"])
                    wait_apart(pool, s["y_ok"], YOK0 + g + 1, s["pool_passed"])
                else:
                    added(t, p, 0)
                nc.gpsimd.indirect_dma_start(m["routed"], bass.IndirectOffsetOnAxis(sidx[:, p % 2, e:e + 1], 0),
                                             ys[SLOTS * e:SLOTS * (e + 1), p % 2, :], None, compute_op=ALU.add).then_inc(s["scat"], 16)

            def shift(t, n):
                g = t * NT + n
                if n % NS == 0:
                    values(t, n // NS)
                pool.wait_ge(s["m_done"], g + 1)
                step = STEPS[n % NS]
                k = len(step[1])
                z = seg(z_buf[:, n % 4], step)
                nc.gpsimd.tensor_tensor(z, z, m_buf[:, n % 8, 0:k].unsqueeze(2).to_broadcast([P, k, P * (step[0] + 1)]),
                                        ALU.subtract).then_inc(s["u_ready"], 1)

            def experts(t, n):
                q, r = n % PAIR_AT, n // PAIR_AT
                if q == 0:
                    gather(t, r)
                if q == 7:
                    scatter(t, r, 0)
                if q == 8:
                    scatter(t, r, 1)
                if q == 9:
                    added(t, r, 1)

            trips(pool, 2, ((2, shift), (0, experts)))

        @block.scalar
        def _(act):
            nc.scalar.preload_act_table_set(ACT_SET)

            act.sem_inc(s["p_done"], PD0)

            def log(t, n):
                g = t * NT + n
                step = STEPS[n % NS]
                ge(act, s["z_done"], g - 1)
                act.wait_ge(s["d_ready"], g + 1)
                nc.scalar.activation(seg(r_buf[:, n % 2], step), seg(ps_d, step), ACT.Ln, scale=-2.0).then_inc(s["ln_done"], 1)

            def root(t, n):
                g = t * NT + n
                step = STEPS[n % NS]
                r = seg(r_buf[:, n % 2], step)
                act.wait_ge(s["ln_done"], g + 1)
                nc.scalar.activation(r, r, ACT.Exp, scale=-0.5).then_inc(s["r_ready"], 1)

            def probs(t, n):
                g = t * NT + n
                step = STEPS[n % NS]
                i, heads, _ = step
                u = unit_of(n)
                act.wait_ge(s["t_ready"], g + 1)
                act.wait_ge(s["pv_done"], PV0 + t * 16 + u - 1)
                nc.scalar.activation(p_buf[:, u % 2, heads[0]:heads[-1] + 1, 0:P * (i + 1)], seg(ps_t, step),
                                     ACT.Exp).then_inc(s["p_done"], 1)

            def experts(t, n, at):
                g = t * 4 + n // PAIR_AT
                if at == 0:
                    act.wait_ge(s["gu_ps"], g + 1)
                    nc.scalar.activation(h_a[:], ps_m[:, 128:128 + F], ACT.Exp, scale=-1.0).then_inc(s["gu_exp"], 1)
                if at == 1:
                    act.wait_ge(s["gu_exp"], g * 3 + 1)
                    nc.scalar.activation(h_a[:], h_a[:], ACT.Ln, bias=one[:]).then_inc(s["gu_exp"], 1)
                if at == 2:
                    act.wait_ge(s["gu_exp"], g * 3 + 2)
                    nc.scalar.activation(h_a[:], h_a[:], ACT.Exp, scale=-1.0).then_inc(s["gu_exp"], 1)

            def sigmoid(q, at):
                return lambda t, n: experts(t, n, at) if n % PAIR_AT == q else None

            act.wait_ge(s["ones"], 1)
            trips(act, LEAD, ((LEAD, log), (0, sigmoid(4, 1)), (0, probs), (0, sigmoid(4, 2)), (LEAD, root),
                              (0, sigmoid(3, 0))))

        @block.tensor
        def _(pe):
            pe.sem_inc(s["pv_done"], PV0)
            pe.sem_inc(s["y_ps"], YPS0)

            def products(out, qs, t, n):
                g = t * NT + n
                par, (i, heads, pitch) = n // NS, STEPS[n % NS]
                w = P * (i + 1)
                for a, c in enumerate(heads):
                    for k0 in range(0, w, CH):
                        k1 = min(w, k0 + CH)
                        diag = out is ps_d and k1 == w
                        last = nc.tensor.matmul(out[:, a * pitch + k0:a * pitch + k1], qs[:, par, c, i * P:(i + 1) * P],
                                                k_t[:, par, c, k0:k1], start=True, stop=not diag)
                        if diag:
                            last = nc.tensor.matmul(out[:, a * pitch + w - P:a * pitch + w], m["identb"][:], m["mask_d"][:],
                                                    start=False, stop=True)
                return last

            def distances(t, n):
                if n % NS == 0:
                    pe.wait_ge(s["ld%d" % (n // NS)], (t + 1) * 16 * LOADS)
                ge(pe, s["ln_done"], t * NT + n)
                products(ps_d, q_d, t, n).then_inc(s["d_ready"], 1)

            def scores(t, n):
                ge(pe, s["z_done"], t * NT + n)
                products(ps_s, q_s, t, n).then_inc(s["s_ready"], 1)

            def values(t, n):
                par = n // NS
                for i, j0, j1 in VALUES[n % NS]:
                    u = 8 * par + QT - 1 - i
                    if j0 == 0:
                        end = par * NS + max(a for a in range(NS) if STEPS[a][0] == i)
                        pe.wait_ge(s["p_done"], PD0 + t * NT + end + 1)
                        if i == QT - 1:
                            pe.wait_ge(s["v_loaded"], t * 2 + par + 1)
                        if i % 4 == 3:
                            pe.wait_ge(s["o_out"], t * 4 + u // 4 + 1)
                    for j in range(j0, j1):
                        for c in range(GH):
                            last = nc.tensor.matmul(ps_o[32 * c:32 * c + 32, (i % 4) * P:(i % 4 + 1) * P],
                                                    v_aug[:, par, j, c, :], p_buf[:, u % 2, c, j * P:(j + 1) * P],
                                                    start=j == 0, stop=j == i)
                    if j1 == i + 1:
                        last.then_inc(s["pv_done"], 1)

            def turn(t, n):
                g = t * NT + n
                i, heads, pitch = STEPS[n % NS]
                pe.wait_ge(s["u_ready"], g + 1)
                pe.wait_ge(s["p_done"], PD0 + g)
                for a in range(len(heads)):
                    for j in range(i + 1):
                        o = a * pitch + j * P
                        diag = j == i
                        last = nc.tensor.matmul(ps_t[:, o:o + P], z_buf[:, n % 4, o:o + P], m["ident"][:], start=True,
                                                stop=not diag, is_transpose=True)
                        if diag:
                            last = nc.tensor.matmul(ps_t[:, o:o + P], m["identb"][:], m["mask_t"][:], start=False, stop=True)
                last.then_inc(s["t_ready"], 1)

            def experts(t, n):
                q, p = n % PAIR_AT, n // PAIR_AT
                g = t * 4 + p
                if q == 2:
                    pe.wait_ge(s["x_got%d" % (p % 2)], 16 * (t * 2 + p // 2 + 1))
                    pe.wait_ge(s["y_ok"], YOK0 + g)
                    nc.tensor.transpose(ps_m[:, 0:P], xg[:, p % 2, 0:D], m["ident"][:]).then_inc(s["xT_ps"], 1)
                if q == 3:
                    pe.wait_ge(s["ld_w%d" % (p % 2)], 32 * (t * 2 + p // 2 + 1))
                    pe.wait_ge(s["xT_ok"], g + 1)
                    for e in range(2):
                        last = nc.tensor.matmul(ps_m[SLOTS * e:SLOTS * (e + 1), 128:128 + 2 * F],
                                                xgT[:, SLOTS * e:SLOTS * (e + 1)], w_gu[:, p % 2, e, :], start=True, stop=True)
                    last.then_inc(s["gu_ps"], 1)
                if q == 5:
                    pe.wait_ge(s["h_step"], g * 3 + 3)
                    nc.tensor.transpose(ps_m[0:F, 320:448], h_a[:], m["ident"][:]).then_inc(s["hT_ps"], 1)
                if q == 6:
                    pe.wait_ge(s["hT_ok"], g + 1)
                    for e in range(2):
                        last = nc.tensor.matmul(ps_m[SLOTS * e:SLOTS * (e + 1), 0:D], hT[:, SLOTS * e:SLOTS * (e + 1)],
                                                w_dn[:, p % 2, e, :], start=True, stop=True)
                    last.then_inc(s["y_ps"], 1)

            trips(pe, LEAD, ((LEAD, distances), (LEAD - 1, scores), (0, turn), (0, values), (0, experts)))

        @block.vector
        def _(dve):
            dve.sem_inc(s["o_out"], 1)
            nc.vector.memset(one[:], 1.0).then_inc(s["ones"], 1)
            dve.sem_inc(s["y_ok"], YOK0)
            for hh in range(2):
                dve.sem_inc(s["o_stored%d" % hh], 16 * (GH + 1))

            def ratios(t, n):
                g = t * NT + n
                step = STEPS[n % NS]
                dve.wait_ge(s["r_ready"], g + 1)
                dve.wait_ge(s["s_ready"], g + 1)
                nc.vector.tensor_tensor(seg(z_buf[:, n % 4], step), seg(ps_s, step), seg(r_buf[:, n % 2], step),
                                        ALU.mult).then_inc(s["z_done"], 1)

            def squares(t, n):
                g = t * NT + n
                step = STEPS[n % NS]
                wait_apart(dve, s["z_done"], g + 1, s["dve_passed"])
                z = seg(z_buf[:, n % 4], step)
                for a in range(len(step[1])):
                    last = nc.vector.tensor_tensor_reduce(out=z[:, a], in0=z[:, a], in1=z[:, a], scale=m["scale"][:], scalar=0.0,
                                                          op0=ALU.mult, op1=ALU.max, accum_out=m_buf[:, n % 8, a:a + 1])
                last.then_inc(s["m_done"], 1)

            def sums_out(t, n):
                par, hh = n // NS, HALF_END.index(n % NS)
                dve.wait_ge(s["pv_done"], PV0 + t * 16 + 8 * par + 4 * hh + 4)
                dve.wait_ge(s["o_stored%d" % hh], 16 * (GH + 1) * (2 * t + par + 1))
                nc.vector.tensor_copy(o_n[:, hh], ps_o[:]).then_inc(s["o_out"], 1)

            def experts(t, n):
                q, p = n % PAIR_AT, n // PAIR_AT
                g = t * 4 + p
                if q == 2:
                    dve.wait_ge(s["xT_ps"], g + 1)
                    nc.vector.tensor_copy(xgT[:], ps_m[:, 0:P]).then_inc(s["xT_ok"], 1)
                if q == 4:
                    dve.wait_ge(s["gu_exp"], g * 3 + 3)
                    nc.vector.tensor_tensor(h_b[:], ps_m[:, 128:128 + F], h_a[:], ALU.mult).then_inc(s["h_step"], 1)
                    dve.wait_ge(s["h_step"], g * 3 + 1)
                    for e in range(2):
                        a, b = SLOTS * e, SLOTS * (e + 1)
                        nc.vector.scalar_tensor_tensor(h_a[a:b], ps_m[a:b, 128 + F:128 + 2 * F],
                                                       xg[a:b, p % 2, bass.ds(D + 2 * g + e, 1)], h_b[a:b],
                                                       ALU.mult, ALU.mult).then_inc(s["h_step"], 1)
                if q == 5:
                    dve.wait_ge(s["hT_ps"], g + 1)
                    nc.vector.tensor_copy(hT[:], ps_m[0:F, 320:448]).then_inc(s["hT_ok"], 1)
                if q == 6:
                    dve.wait_ge(s["y_ps"], YPS0 + g + 1)
                    nc.vector.tensor_copy(ys[:, p % 2], ps_m[:, 0:D]).then_inc(s["y_ok"], 1)

            def rest(t, n):
                if n % NS in HALF_END:
                    sums_out(t, n)
                experts(t, n)

            trips(dve, LEAD - 1, ((LEAD - 1, ratios), (LEAD - 1, squares), (0, rest)))


def output(nc, m, out):
    with ExitStack() as ctx:
        def sb(name, shape, dt=F32):
            return ctx.enter_context(nc.sbuf_tensor(name, shape, dt))

        def ps(name, shape):
            return ctx.enter_context(nc.psum_tensor(name, shape, F32))

        w_o, w_sgu, w_sdn = m["w_o"], m["w_sgu"], m["w_sdn"]
        a_t = sb("a_t", [P, 2, CH])
        s_t = sb("s_t", [P, 2, CH])
        a_n = sb("a_n", [P, 2, CH])
        r_r = sb("r_r", [P, 2, 4, D])
        sg = sb("sg", [F, 2, CH])
        sg1 = sb("sg1", [F, 2, CH])
        h_t = sb("h_t", [F, 2, CH])
        acc = sb("acc", [P, 2, 4, D])
        res = sb("res_out", [P, 2, 4, D])
        psg = ps("psg", [P, 2, CH])
        psu = ps("psu", [P, 2, CH])
        psy = ps("psy", [P, 2, CH])
        one = sb("one_out", [P, 1])
        s = {n: ctx.enter_context(nc.semaphore("c_" + n)) for n in
             "ld_a0 ld_a1 ld_r0 ld_r1 inv norm gu ex hs y add sum one stored0 stored1 passed".split()}
        block = ctx.enter_context(nc.Block())

        def chunks(eng, chunk):
            with eng.Fori(0, B) as b:
                for hf in range(2):
                    chunk(b, hf)

        @block.sync
        def _(sp):
            def load_att(b, hf):
                src = m["att_d"][bass.ds(2 * b, 2), :, :, hf * CH:(hf + 1) * CH].rearrange("g p r q -> (g p r) q")
                sp.dma_start(a_t[:, hf], src).then_inc(s["ld_a%d" % hf], 16)
                src = m["sums_d"][bass.ds(2 * b, 2), :, :, hf * CH:(hf + 1) * CH].rearrange("g p c q -> (g p c) q")
                sp.dma_start(s_t[:, hf], src.unsqueeze(1).to_broadcast([H, HD, CH])).then_inc(s["ld_a%d" % hf], 16)

            def load_routed(b, hf):
                src = m["routed"][bass.ds((2 * b + hf) * CH, CH), :]
                sp.dma_start(r_r[:, hf], src.rearrange("(n p) d -> p n d", p=P)).then_inc(s["ld_r%d" % hf], 16)

            def store(b, hf):
                g = b * 2 + hf
                wait_apart(sp, s["sum"], g + 3, s["passed"])
                dst = out[bass.ds(g * CH, CH), :].rearrange("(n p) d -> p n d", p=P)
                sp.dma_start(dst, res[:, hf]).then_inc(s["stored%d" % hf], 16)

            for hf in range(2):
                load_att(0, hf)
                load_routed(0, hf)
            for hh in range(2):
                sp.wait_ge(m["o_stored%d" % hh], 16 * (GH + 1) * (1 + 2 * TRIPS))
            with sp.Fori(0, B - 1) as b:
                for hf in range(2):
                    g = b * 2 + hf
                    wait_apart(sp, s["add"], g + 1, s["passed"])
                    load_routed(b + 1, hf)
                    wait_apart(sp, s["norm"], g + 1, s["passed"])
                    load_att(b + 1, hf)
                    store(b, hf)
            for hf in range(2):
                store(B - 1, hf)
            for hf in range(2):
                sp.wait_ge(s["stored%d" % hf], 16 * (B + 1))

        @block.scalar
        def _(act):
            nc.scalar.preload_act_table_set(ACT_SET)
            act.wait_ge(s["one"], 1)

            def sigmoid(b, hf):
                g = b * 2 + hf
                act.wait_ge(s["hs"], 2 * g + 2)
                act.wait_ge(s["gu"], g + 1)
                nc.scalar.activation(sg[:, hf], psg[0:F, hf], ACT.Exp, scale=-1.0).then_inc(s["ex"], 1)
                act.wait_ge(s["ex"], 3 * g + 1)
                nc.scalar.activation(sg[:, hf], sg[:, hf], ACT.Ln, bias=one[0:F]).then_inc(s["ex"], 1)
                act.wait_ge(s["ex"], 3 * g + 2)
                nc.scalar.activation(sg1[:, hf], sg[:, hf], ACT.Exp, scale=-1.0).then_inc(s["ex"], 1)
                act.wait_ge(s["ld_a%d" % hf], 32 * (b + 1))
                nc.scalar.activation(s_t[:, hf], s_t[:, hf], ACT.Ln).then_inc(s["inv"], 1)
                act.wait_ge(s["inv"], 2 * g + 1)
                nc.scalar.activation(s_t[:, hf], s_t[:, hf], ACT.Exp, scale=-1.0).then_inc(s["inv"], 1)

            chunks(act, sigmoid)

        @block.gpsimd
        def _(pool):
            def add(b, hf):
                g = b * 2 + hf
                pool.wait_ge(s["sum"], g + 1)
                pool.wait_ge(s["ld_r%d" % hf], 16 * (b + 1))
                nc.gpsimd.tensor_tensor(acc[:, hf], m["x_all"][:, bass.ds(4 * g, 4), :], r_r[:, hf], ALU.add).then_inc(s["add"], 1)

            chunks(pool, add)

        @block.tensor
        def _(pe):
            def gates(b, hf):
                g = b * 2 + hf
                pe.wait_ge(s["hs"], 2 * g + 2)
                nc.tensor.matmul(psg[0:F, hf], w_sgu[:, 0:F], m["xT_all"][:, bass.ds(g * CH, CH)], start=True, stop=True)
                nc.tensor.matmul(psu[0:F, hf], w_sgu[:, F:2 * F], m["xT_all"][:, bass.ds(g * CH, CH)], start=True, stop=True).then_inc(s["gu"], 1)

            def rows(b, hf):
                g = b * 2 + hf
                pe.wait_ge(s["hs"], 4 + 2 * g + 2)
                pe.wait_ge(s["norm"], g + 1)
                pe.wait_ge(s["sum"], g + 1)
                for i in range(4):
                    o = psy[:, hf, i * P:(i + 1) * P]
                    nc.tensor.matmul(o, a_n[:, hf, i * P:(i + 1) * P], w_o[:], start=True, stop=False)
                    last = nc.tensor.matmul(o, h_t[:, hf, i * P:(i + 1) * P], w_sdn[:], start=False, stop=True)
                last.then_inc(s["y"], 1)

            gates(0, 0)
            with pe.Fori(0, B - 1) as b:
                gates(b, 1)
                rows(b, 0)
                gates(b + 1, 0)
                rows(b, 1)
            gates(B - 1, 1)
            rows(B - 1, 0)
            rows(B - 1, 1)

        @block.vector
        def _(dve):
            dve.sem_inc(s["hs"], 4)
            dve.sem_inc(s["sum"], 2)
            for hf in range(2):
                dve.sem_inc(s["stored%d" % hf], 16)
            nc.vector.memset(one[:], 1.0).then_inc(s["one"], 1)

            def hidden(b, hf):
                g = b * 2 + hf
                dve.wait_ge(s["ex"], 3 * g + 3)
                if not isinstance(g, int) or g > 1:
                    dve.wait_ge(s["y"], g - 1)
                nc.vector.tensor_tensor(h_t[:, hf], psg[0:F, hf], sg1[:, hf], ALU.mult).then_inc(s["hs"], 1)
                dve.wait_ge(s["hs"], 4 + 2 * g + 1)
                nc.vector.tensor_tensor(h_t[:, hf], psu[0:F, hf], h_t[:, hf], ALU.mult).then_inc(s["hs"], 1)
                dve.wait_ge(s["inv"], 2 * g + 2)
                nc.vector.tensor_tensor(a_n[:, hf], a_t[:, hf], s_t[:, hf], ALU.mult).then_inc(s["norm"], 1)

            def total(b, hf):
                g = b * 2 + hf
                dve.wait_ge(s["stored%d" % hf], 16 * (b + 1))
                dve.wait_ge(s["add"], g + 1)
                dve.wait_ge(s["y"], g + 1)
                nc.vector.tensor_tensor(res[:, hf], psy[:, hf].rearrange("p (n d) -> p n d", n=4), acc[:, hf],
                                        ALU.add).then_inc(s["sum"], 1)

            hidden(0, 0)
            hidden(0, 1)
            total(0, 0)
            with dve.Fori(1, B) as b:
                hidden(b, 0)
                total(b - 1, 1)
                hidden(b, 1)
                total(b, 0)
            total(B - 1, 1)


def kernel(L0_attn_x, L0_attn_Wq, L0_attn_Wk, L0_attn_Wv, L0_attn_Wo, L0_attn_alpha, L0_ffn_router_w, L0_ffn_w_gate,
           L0_ffn_w_up, L0_ffn_w_down, L0_ffn_ws_gate_up, L0_ffn_ws_down):
    import concourse.bacc as bacc
    from concourse.bass_utils import run_bass_kernel_spmd

    def a(v):
        return np.ascontiguousarray(np.asarray(v))

    other = np.arange(D) ^ 1
    consts = np.zeros((P, 449), np.float32)
    row, col = np.arange(P)[:, None], np.arange(P)[None, :]
    consts[:, 0:P] = np.eye(P)
    consts[:, 128:256] = np.where(col > row, np.float32(MASK_D), 0)
    consts[:, 256:384] = np.where(row > col, np.float32(MASK_T), 0)
    consts[:, 384:400] = np.where(row // HD == np.arange(16)[None, :], -0.5, 0)
    consts[:, 416:448] = T - (np.arange(TILES)[None, :] * P + row)
    consts[:, 448] = np.arange(P) % SLOTS
    freq = np.outer(1.0 / 10000.0 ** (np.arange(0, HD, 2)[:HD // 2] / HD), np.arange(S))
    pair = (np.arange(P) % HD) // 2
    sign = np.where(np.arange(P) % 2 == 0, -1.0, 1.0)[:, None]
    rope = np.stack([np.cos(freq)[pair], sign * np.sin(freq)[pair]], 1).astype(np.float32)

    x = a(L0_attn_x).reshape(T, D)
    wq, wk = a(L0_attn_Wq), a(L0_attn_Wk)
    ins = {
        "x": x, "wq": wq, "wqs": a(wq[:, other]), "wk": wk, "wks": a(wk[:, other]), "wv": a(L0_attn_Wv),
        "wo": a(L0_attn_Wo), "alpha": a(np.broadcast_to(a(L0_attn_alpha), (P, 1))), "rwt": a(a(L0_ffn_router_w).T),
        "wgu": a(np.concatenate([a(L0_ffn_w_gate), a(L0_ffn_w_up)], 2)), "wdn": a(L0_ffn_w_down),
        "wsgu": a(L0_ffn_ws_gate_up), "wsdn": a(L0_ffn_ws_down), "consts": consts, "rope": a(rope),
    }
    nc = bacc.Bacc("TRN2", target_bir_lowering=False, num_devices=1)
    aps = {n: nc.dram_tensor("in_" + n, list(v.shape), mybir.dt.from_np(v.dtype), kind="ExternalInput").ap()
           for n, v in ins.items()}
    out = nc.dram_tensor("out", [T, D], F32, kind="ExternalOutput").ap()
    program(nc, out=out, **aps)
    r = run_bass_kernel_spmd(nc, [{"in_" + n: v for n, v in ins.items()}], core_ids=[0])
    return r.results[0]["out"].reshape(B, S, D)
```
